# Optimizing a Trainium2 kernel written in Bass

```python
import numpy as np
import jax
import jax.numpy as jnp

def _softmax(x, axis=-1):
    return jax.nn.softmax(x, axis=axis)
def _gelu(x):
    return jax.nn.gelu(x, approximate=True)
def _silu(x):
    return jax.nn.silu(x)
def _sigmoid(x):
    return jax.nn.sigmoid(x)
def _layernorm(x, axis=-1, eps=1e-5):
    m = jnp.mean(x, axis=axis, keepdims=True)
    v = jnp.var(x, axis=axis, keepdims=True)
    return (x - m) / jnp.sqrt(v + eps)
def _scatter_add(tgt, idx, src, axis=0):
    return tgt.at[idx].add(src)
def _segment_sum(src, seg, n):
    return jax.ops.segment_sum(src, seg, n)

kernel_name = 'mk_conv_attn_hybrid_d4_conv_nhwc128_ada13d'

def setup_inputs(seed: int = 0):
    np.random.seed(seed)
    _w = jnp.asarray
    def _rec_inputs():
        import jax
        import jax.numpy as jnp
        _gk = jax.random.key(seed)
        x = -0.0005153 + 1.001 * jax.random.normal(jax.random.fold_in(_gk, 1), (8, 56, 56, 128), jnp.float32)
        return x
    x = _rec_inputs()
    def _L0_conv_setup():
        import jax, jax.numpy as jnp
        import numpy as np
        KH = KW = 3
        PAD = 1
        DIL = 1
        GROUP = 4
        OFFSET_SCALE = 1.0
        P = KH * KW

        def bilinear_sample(img, iy, ix, H, W):
            x0 = jnp.floor(ix)
            y0 = jnp.floor(iy)
            wx1 = ix - x0
            wy1 = iy - y0

            def corner(yf, xf, wgt):
                valid = (yf >= 0) & (yf < H) & (xf >= 0) & (xf < W)
                idx = jnp.clip(yf, 0, H - 1).astype(jnp.int32) * W + jnp.clip(xf, 0, W - 1).astype(jnp.int32)
                v = jax.vmap(lambda im, i: im[i])(img, idx)
                return v * (wgt * valid)[..., None]
            return corner(y0, x0, (1 - wy1) * (1 - wx1)) + corner(y0, x0 + 1, (1 - wy1) * wx1) + corner(y0 + 1, x0, wy1 * (1 - wx1)) + corner(y0 + 1, x0 + 1, wy1 * wx1)

        def dcn_core(x_proj, offset, mask_sm):
            N, H, W, C = x_proj.shape
            Hin, Win = (H + 2 * PAD, W + 2 * PAD)
            Cg = C // GROUP
            pad = jnp.pad(x_proj, ((0, 0), (PAD, PAD), (PAD, PAD), (0, 0)))
            img = pad.reshape(N, Hin, Win, GROUP, Cg).transpose(0, 3, 1, 2, 4).reshape(N * GROUP, Hin * Win, Cg)
            ref_x = (jnp.arange(W, dtype=jnp.float32) + DIL * (KW - 1) // 2 + 0.5) / Win
            ref_y = (jnp.arange(H, dtype=jnp.float32) + DIL * (KH - 1) // 2 + 0.5) / Hin
            gx = jnp.arange(KW, dtype=jnp.float32) * DIL - DIL * (KW - 1) // 2
            gy = jnp.arange(KH, dtype=jnp.float32) * DIL - DIL * (KH - 1) // 2
            gxx, gyy = jnp.meshgrid(gx, gy, indexing='ij')
            gpx = (gxx / Win).reshape(P)
            gpy = (gyy / Hin).reshape(P)
            loc_x = ref_x[None, None, :, None, None] + gpx[None, None, None, None, :] * OFFSET_SCALE + offset[..., 0] * (OFFSET_SCALE / Win)
            loc_y = ref_y[None, :, None, None, None] + gpy[None, None, None, None, :] * OFFSET_SCALE + offset[..., 1] * (OFFSET_SCALE / Hin)
            ix = (loc_x * Win - 0.5).transpose(0, 3, 1, 2, 4).reshape(N * GROUP, H * W * P)
            iy = (loc_y * Hin - 0.5).transpose(0, 3, 1, 2, 4).reshape(N * GROUP, H * W * P)
            samp = bilinear_sample(img, iy, ix, Hin, Win)
            samp = samp.reshape(N, GROUP, H, W, P, Cg)
            return jnp.einsum('nghwpc,nhwgp->nhwgc', samp, mask_sm).reshape(N, H, W, C)

        def layer_norm(z, g, b, eps=1e-05):
            m = z.mean(-1, keepdims=True)
            v = ((z - m) ** 2).mean(-1, keepdims=True)
            return (z - m) / jnp.sqrt(v + eps) * g + b
        key = jax.random.key(seed)
        ks = jax.random.split(key, 12)
        N, H, W, C, G, R = (8, 56, 56, 128, GROUP, 4)

        def w(k, shp, s=0.02):
            return jax.random.normal(k, shp, jnp.float32) * s
        return dict(x=jax.random.normal(ks[0], (N, H, W, C), jnp.float32), w_in=w(ks[1], (C, C)), b_in=jnp.zeros((C,), jnp.float32), dw_w=w(ks[2], (C, 1, KH, KW)), dw_b=jnp.zeros((C,), jnp.float32), bn_g=jnp.ones((C,), jnp.float32), bn_b=jnp.zeros((C,), jnp.float32), bn_m=w(ks[3], (C,), 0.1), bn_v=jax.random.uniform(ks[4], (C,), jnp.float32, 0.5, 1.5), w_off=w(ks[5], (C, G * P * 2)), b_off=jnp.zeros((G * P * 2,), jnp.float32), w_msk=w(ks[6], (C, G * P)), b_msk=jnp.zeros((G * P,), jnp.float32), w_out=w(ks[7], (C, C)), b_out=jnp.zeros((C,), jnp.float32), ln1_g=jnp.ones((C,), jnp.float32), ln1_b=jnp.zeros((C,), jnp.float32), w_fc1=w(ks[8], (C, R * C)), b_fc1=jnp.zeros((R * C,), jnp.float32), w_fc2=w(ks[9], (R * C, C)), b_fc2=jnp.zeros((C,), jnp.float32), ln2_g=jnp.ones((C,), jnp.float32), ln2_b=jnp.zeros((C,), jnp.float32), gamma1=jnp.ones((C,), jnp.float32), gamma2=jnp.ones((C,), jnp.float32))
    _L0_conv_all = _L0_conv_setup()
    _L0_conv_in = {k: v for k, v in _L0_conv_all.items() if k in ('w_in', 'b_in', 'dw_w', 'dw_b', 'bn_g', 'bn_b', 'bn_m', 'bn_v', 'w_off', 'b_off', 'w_msk', 'b_msk', 'w_out', 'b_out', 'ln1_g', 'ln1_b', 'w_fc1', 'b_fc1', 'w_fc2', 'b_fc2', 'ln2_g', 'ln2_b', 'gamma1', 'gamma2', )}
    del _L0_conv_all

    def _L1_conv_setup():
        import jax, jax.numpy as jnp
        import numpy as np
        KSIZE, CIN, COUT = (3, 128, 128)
        OFF_X, OFF_Y = (1, 1)
        B, H, W_ = (8, 256, 256)
        key = jax.random.key(seed)
        k_in, k_w = jax.random.split(key)
        inputs = jax.random.normal(k_in, (B, H, W_, CIN), dtype=jnp.float32)
        kernel = jnp.zeros((KSIZE, KSIZE, CIN, COUT), dtype=jnp.float32)
        kernel = kernel.at[OFF_X, OFF_Y].set(jnp.ones((CIN, COUT), dtype=jnp.float32))
        bias = jnp.zeros((COUT,), dtype=jnp.float32)
        Wd = jax.random.normal(k_w, (COUT, COUT), dtype=jnp.float32) * (1.0 / np.sqrt(COUT))
        return {'inputs': inputs, 'kernel': kernel, 'bias': bias, 'W': Wd}
    _L1_conv_all = _L1_conv_setup()
    _L1_conv_in = {k: v for k, v in _L1_conv_all.items() if k in ('kernel', 'bias', 'W', )}
    del _L1_conv_all

    def _L2_attn_setup():
        import jax, jax.numpy as jnp
        import numpy as np
        B, N, D = (4, 1024, 128)
        key = jax.random.key(seed)
        ks = jax.random.split(key, 4)
        scale = 1.0 / np.sqrt(D)
        return {'inputs': jax.random.normal(ks[0], (B, N, D), dtype=jnp.float32), 'Wq': jax.random.normal(ks[1], (D, D), dtype=jnp.float32) * scale, 'bq': jnp.zeros((D,), dtype=jnp.float32), 'Wk': jax.random.normal(ks[2], (D, D), dtype=jnp.float32) * scale, 'bk': jnp.zeros((D,), dtype=jnp.float32), 'Wv': jax.random.normal(ks[3], (D, D), dtype=jnp.float32) * scale, 'bv': jnp.zeros((D,), dtype=jnp.float32)}
    _L2_attn_all = _L2_attn_setup()
    _L2_attn_in = {k: v for k, v in _L2_attn_all.items() if k in ('Wq', 'bq', 'Wk', 'bk', 'Wv', 'bv', )}
    del _L2_attn_all

    def _L2_ffn_setup():
        import jax, jax.numpy as jnp
        import numpy as np
        B, S, D, E, H, O, K = (512, 2048, 128, 64, 512, 128, 8)
        key = jax.random.key(seed)
        k0, k1, k2, k3 = jax.random.split(key, 4)
        x = jax.random.normal(k0, (B, S, D), dtype=jnp.float32)
        gate_w = jax.random.normal(k1, (E, D), dtype=jnp.float32) * (1.0 / np.sqrt(D))
        gate_b = jnp.zeros((E,), dtype=jnp.float32)
        weight1 = jax.random.uniform(k2, (E, D + 1, H), dtype=jnp.float32, minval=-1.0, maxval=1.0) * (1.0 / np.sqrt(D + 1))
        weight2 = jax.random.uniform(k3, (E, H + 1, O), dtype=jnp.float32, minval=-1.0, maxval=1.0) * (1.0 / np.sqrt(H + 1))
        return {'x': x, 'gate_w': gate_w, 'gate_b': gate_b, 'weight1': weight1, 'weight2': weight2}
    _L2_ffn_all = _L2_ffn_setup()
    _L2_ffn_in = {k: v for k, v in _L2_ffn_all.items() if k in ('gate_w', 'gate_b', 'weight1', 'weight2', )}
    del _L2_ffn_all

    def _L3_attn_setup():
        import jax, jax.numpy as jnp
        import numpy as np
        key = jax.random.key(seed)
        x = jax.random.normal(key, (4, 4096, 128), dtype=jnp.float32)
        return {'x': x}
    _L3_attn_all = _L3_attn_setup()
    _L3_attn_in = {k: v for k, v in _L3_attn_all.items() if k in ()}
    del _L3_attn_all

    def _L3_ffn_setup():
        import jax, jax.numpy as jnp
        import numpy as np
        B, N, D, C, E, K = (8, 8192, 128, 128, 8, 2)
        key = jax.random.key(seed)
        k0, k1, k2 = jax.random.split(key, 3)
        x = jax.random.normal(k0, (B, N, D), dtype=jnp.float32)
        router_w = jax.random.normal(k1, (D, E), dtype=jnp.float32) * 0.05
        router_b = jnp.zeros((E,), dtype=jnp.float32)
        expert_w = jax.random.normal(k2, (E, D, C), dtype=jnp.float32) * (1.0 / np.sqrt(D))
        expert_b = jnp.zeros((E, C), dtype=jnp.float32)
        return {'x': x, 'router_w': router_w, 'router_b': router_b, 'expert_w': expert_w, 'expert_b': expert_b}
    _L3_ffn_all = _L3_ffn_setup()
    _L3_ffn_in = {k: v for k, v in _L3_ffn_all.items() if k in ('router_w', 'router_b', 'expert_w', 'expert_b', )}
    del _L3_ffn_all

    return {
        "x": x,
        "L0_conv_w_in": _L0_conv_in["w_in"],
        "L0_conv_b_in": _L0_conv_in["b_in"],
        "L0_conv_dw_w": _L0_conv_in["dw_w"],
        "L0_conv_dw_b": _L0_conv_in["dw_b"],
        "L0_conv_bn_g": _L0_conv_in["bn_g"],
        "L0_conv_bn_b": _L0_conv_in["bn_b"],
        "L0_conv_bn_m": _L0_conv_in["bn_m"],
        "L0_conv_bn_v": _L0_conv_in["bn_v"],
        "L0_conv_w_off": _L0_conv_in["w_off"],
        "L0_conv_b_off": _L0_conv_in["b_off"],
        "L0_conv_w_msk": _L0_conv_in["w_msk"],
        "L0_conv_b_msk": _L0_conv_in["b_msk"],
        "L0_conv_w_out": _L0_conv_in["w_out"],
        "L0_conv_b_out": _L0_conv_in["b_out"],
        "L0_conv_ln1_g": _L0_conv_in["ln1_g"],
        "L0_conv_ln1_b": _L0_conv_in["ln1_b"],
        "L0_conv_w_fc1": _L0_conv_in["w_fc1"],
        "L0_conv_b_fc1": _L0_conv_in["b_fc1"],
        "L0_conv_w_fc2": _L0_conv_in["w_fc2"],
        "L0_conv_b_fc2": _L0_conv_in["b_fc2"],
        "L0_conv_ln2_g": _L0_conv_in["ln2_g"],
        "L0_conv_ln2_b": _L0_conv_in["ln2_b"],
        "L0_conv_gamma1": _L0_conv_in["gamma1"],
        "L0_conv_gamma2": _L0_conv_in["gamma2"],
        "L1_conv_kernel": _L1_conv_in["kernel"],
        "L1_conv_bias": _L1_conv_in["bias"],
        "L1_conv_W": _L1_conv_in["W"],
        "L2_attn_Wq": _L2_attn_in["Wq"],
        "L2_attn_bq": _L2_attn_in["bq"],
        "L2_attn_Wk": _L2_attn_in["Wk"],
        "L2_attn_bk": _L2_attn_in["bk"],
        "L2_attn_Wv": _L2_attn_in["Wv"],
        "L2_attn_bv": _L2_attn_in["bv"],
        "L2_ffn_gate_w": _L2_ffn_in["gate_w"],
        "L2_ffn_gate_b": _L2_ffn_in["gate_b"],
        "L2_ffn_weight1": _L2_ffn_in["weight1"],
        "L2_ffn_weight2": _L2_ffn_in["weight2"],
        "L3_ffn_router_w": _L3_ffn_in["router_w"],
        "L3_ffn_router_b": _L3_ffn_in["router_b"],
        "L3_ffn_expert_w": _L3_ffn_in["expert_w"],
        "L3_ffn_expert_b": _L3_ffn_in["expert_b"],
    }

def reference(x, L0_conv_w_in, L0_conv_b_in, L0_conv_dw_w, L0_conv_dw_b, L0_conv_bn_g, L0_conv_bn_b, L0_conv_bn_m, L0_conv_bn_v, L0_conv_w_off, L0_conv_b_off, L0_conv_w_msk, L0_conv_b_msk, L0_conv_w_out, L0_conv_b_out, L0_conv_ln1_g, L0_conv_ln1_b, L0_conv_w_fc1, L0_conv_b_fc1, L0_conv_w_fc2, L0_conv_b_fc2, L0_conv_ln2_g, L0_conv_ln2_b, L0_conv_gamma1, L0_conv_gamma2, L1_conv_kernel, L1_conv_bias, L1_conv_W, L2_attn_Wq, L2_attn_bq, L2_attn_Wk, L2_attn_bk, L2_attn_Wv, L2_attn_bv, L2_ffn_gate_w, L2_ffn_gate_b, L2_ffn_weight1, L2_ffn_weight2, L3_ffn_router_w, L3_ffn_router_b, L3_ffn_expert_w, L3_ffn_expert_b):
    import jax
    import jax.numpy as jnp
    def _L0_conv_ref(x, w_in, b_in, dw_w, dw_b, bn_g, bn_b, bn_m, bn_v, w_off, b_off, w_msk, b_msk, w_out, b_out, ln1_g, ln1_b, w_fc1, b_fc1, w_fc2, b_fc2, ln2_g, ln2_b, gamma1, gamma2):
        import jax, jax.numpy as jnp
        import numpy as np
        KH = KW = 3
        PAD = 1
        DIL = 1
        GROUP = 4
        OFFSET_SCALE = 1.0
        P = KH * KW

        def bilinear_sample(img, iy, ix, H, W):
            x0 = jnp.floor(ix)
            y0 = jnp.floor(iy)
            wx1 = ix - x0
            wy1 = iy - y0

            def corner(yf, xf, wgt):
                valid = (yf >= 0) & (yf < H) & (xf >= 0) & (xf < W)
                idx = jnp.clip(yf, 0, H - 1).astype(jnp.int32) * W + jnp.clip(xf, 0, W - 1).astype(jnp.int32)
                v = jax.vmap(lambda im, i: im[i])(img, idx)
                return v * (wgt * valid)[..., None]
            return corner(y0, x0, (1 - wy1) * (1 - wx1)) + corner(y0, x0 + 1, (1 - wy1) * wx1) + corner(y0 + 1, x0, wy1 * (1 - wx1)) + corner(y0 + 1, x0 + 1, wy1 * wx1)

        def dcn_core(x_proj, offset, mask_sm):
            N, H, W, C = x_proj.shape
            Hin, Win = (H + 2 * PAD, W + 2 * PAD)
            Cg = C // GROUP
            pad = jnp.pad(x_proj, ((0, 0), (PAD, PAD), (PAD, PAD), (0, 0)))
            img = pad.reshape(N, Hin, Win, GROUP, Cg).transpose(0, 3, 1, 2, 4).reshape(N * GROUP, Hin * Win, Cg)
            ref_x = (jnp.arange(W, dtype=jnp.float32) + DIL * (KW - 1) // 2 + 0.5) / Win
            ref_y = (jnp.arange(H, dtype=jnp.float32) + DIL * (KH - 1) // 2 + 0.5) / Hin
            gx = jnp.arange(KW, dtype=jnp.float32) * DIL - DIL * (KW - 1) // 2
            gy = jnp.arange(KH, dtype=jnp.float32) * DIL - DIL * (KH - 1) // 2
            gxx, gyy = jnp.meshgrid(gx, gy, indexing='ij')
            gpx = (gxx / Win).reshape(P)
            gpy = (gyy / Hin).reshape(P)
            loc_x = ref_x[None, None, :, None, None] + gpx[None, None, None, None, :] * OFFSET_SCALE + offset[..., 0] * (OFFSET_SCALE / Win)
            loc_y = ref_y[None, :, None, None, None] + gpy[None, None, None, None, :] * OFFSET_SCALE + offset[..., 1] * (OFFSET_SCALE / Hin)
            ix = (loc_x * Win - 0.5).transpose(0, 3, 1, 2, 4).reshape(N * GROUP, H * W * P)
            iy = (loc_y * Hin - 0.5).transpose(0, 3, 1, 2, 4).reshape(N * GROUP, H * W * P)
            samp = bilinear_sample(img, iy, ix, Hin, Win)
            samp = samp.reshape(N, GROUP, H, W, P, Cg)
            return jnp.einsum('nghwpc,nhwgp->nhwgc', samp, mask_sm).reshape(N, H, W, C)

        def layer_norm(z, g, b, eps=1e-05):
            m = z.mean(-1, keepdims=True)
            v = ((z - m) ** 2).mean(-1, keepdims=True)
            return (z - m) / jnp.sqrt(v + eps) * g + b
        N, H, W, C = x.shape
        xp = x @ w_in + b_in
        h = x.transpose(0, 3, 1, 2)
        h = jax.lax.conv_general_dilated(h, dw_w, (1, 1), ((PAD, PAD), (PAD, PAD)), feature_group_count=C, dimension_numbers=('NCHW', 'OIHW', 'NCHW')) + dw_b[None, :, None, None]
        h = (h - bn_m[None, :, None, None]) * (bn_g / jnp.sqrt(bn_v + 1e-05))[None, :, None, None] + bn_b[None, :, None, None]
        h = jax.nn.gelu(h.transpose(0, 2, 3, 1), approximate=False)
        offset = (h @ w_off + b_off).reshape(N, H, W, GROUP, P, 2)
        mask = jax.nn.softmax((h @ w_msk + b_msk).reshape(N, H, W, GROUP, P), axis=-1)
        y = dcn_core(xp, offset, mask) @ w_out + b_out
        x = x + gamma1 * layer_norm(y, ln1_g, ln1_b)
        m = jax.nn.gelu(x @ w_fc1 + b_fc1, approximate=False) @ w_fc2 + b_fc2
        x = x + gamma2 * layer_norm(m, ln2_g, ln2_b)
        return x

    def _L1_conv_ref(inputs, kernel, bias, W):
        import jax, jax.numpy as jnp
        import numpy as np
        KSIZE, CIN, COUT = (3, 128, 128)
        OFF_X, OFF_Y = (1, 1)
        B, H, W_ = (8, 256, 256)
        img = jax.lax.conv_general_dilated(inputs, kernel, window_strides=(1, 1), padding='SAME', dimension_numbers=('NHWC', 'HWIO', 'NHWC')) + bias
        return jnp.einsum('bhwc,co->bhwo', img, W)

    def _L2_attn_ref(inputs, Wq, bq, Wk, bk, Wv, bv):
        import jax, jax.numpy as jnp
        import numpy as np
        B, N, D = (4, 1024, 128)
        q = inputs @ Wq + bq
        k = inputs @ Wk + bk
        v = inputs @ Wv + bv
        kv = jnp.sum(k * v, axis=1, keepdims=True)
        return q * kv

    def _L2_ffn_ref(x, gate_w, gate_b, weight1, weight2):
        import jax, jax.numpy as jnp
        import numpy as np
        B, S, D, E, H, O, K = (512, 2048, 128, 64, 512, 128, 8)
        Bn, Sn, Dn = x.shape
        logits = jnp.einsum('bsd,ed->bse', x, gate_w) + gate_b
        probs = jax.nn.softmax(logits, axis=1)
        vals, idx = jax.lax.top_k(probs.transpose(0, 2, 1), K)
        topv = vals.transpose(0, 2, 1)
        topi = idx.transpose(0, 2, 1)
        flat_idx = topi.reshape(Bn, K * E)
        gathered = jnp.take_along_axis(x, flat_idx[:, :, None], axis=1)
        gathered = gathered.reshape(Bn, K, E, Dn)
        pooled = jnp.einsum('bked,bke->bed', gathered, topv)
        ones = jnp.ones((E, Bn, 1), dtype=x.dtype)
        h = jnp.concatenate([pooled.transpose(1, 0, 2), ones], axis=-1)
        h = jax.nn.gelu(jnp.einsum('ebd,edh->ebh', h, weight1), approximate=False)
        h = jnp.concatenate([h, ones], axis=-1)
        out = jnp.einsum('ebh,eho->ebo', h, weight2)
        out = out.transpose(1, 0, 2)
        weighted = jnp.einsum('beo,bke->bkeo', out, topv).reshape(Bn, K * E, O)
        outputs = jnp.zeros((Bn, Sn, O), dtype=x.dtype)
        outputs = outputs.at[jnp.arange(Bn)[:, None], flat_idx].add(weighted)
        return outputs

    def _L3_attn_ref(x):
        import jax, jax.numpy as jnp
        import numpy as np
        scores = jnp.einsum('bsd,btd->bst', x, x)
        attn_weights = jax.nn.softmax(scores, axis=-1)
        return jnp.einsum('bst,btd->bsd', attn_weights, x)

    def _L3_ffn_ref(x, router_w, router_b, expert_w, expert_b):
        import jax, jax.numpy as jnp
        import numpy as np
        B, N, D, C, E, K = (8, 8192, 128, 128, 8, 2)
        router_probs = jax.nn.softmax(x @ router_w + router_b, axis=-1)
        top_p, top_i = jax.lax.top_k(router_probs, K)
        top_p = top_p / jnp.sum(top_p, axis=-1, keepdims=True)
        expert_out = jnp.einsum('bnd,edc->bnec', x, expert_w) + expert_b
        gathered = jnp.take_along_axis(expert_out, top_i[..., None], axis=2)
        return jnp.einsum('bnk,bnkc->bnc', top_p, gathered)

    def _gn(v, G=32, eps=1e-5):
        B_, H_, W_, C_ = v.shape
        g = v.reshape(B_, H_, W_, G, C_ // G)
        m = jnp.mean(g, axis=(1, 2, 4), keepdims=True)
        s = jnp.var(g, axis=(1, 2, 4), keepdims=True)
        return ((g - m) / jnp.sqrt(s + eps)).reshape(v.shape)

    def _ln_c(v, eps=1e-6):
        m = jnp.mean(v, axis=-1, keepdims=True)
        s = jnp.var(v, axis=-1, keepdims=True)
        return (v - m) / jnp.sqrt(s + eps)

    def _ln_t(v, eps=1e-5):
        m = jnp.mean(v, axis=-1, keepdims=True)
        s = jnp.var(v, axis=-1, keepdims=True)
        return (v - m) / jnp.sqrt(s + eps)

    def _to_tokens(v):
        B_, H_, W_, C_ = v.shape
        return v.reshape(B_, H_ * W_, C_)
    def _from_tokens(t, like):
        return t.reshape(like.shape)

    x = _L0_conv_ref(x, L0_conv_w_in, L0_conv_b_in, L0_conv_dw_w, L0_conv_dw_b, L0_conv_bn_g, L0_conv_bn_b, L0_conv_bn_m, L0_conv_bn_v, L0_conv_w_off, L0_conv_b_off, L0_conv_w_msk, L0_conv_b_msk, L0_conv_w_out, L0_conv_b_out, L0_conv_ln1_g, L0_conv_ln1_b, L0_conv_w_fc1, L0_conv_b_fc1, L0_conv_w_fc2, L0_conv_b_fc2, L0_conv_ln2_g, L0_conv_ln2_b, L0_conv_gamma1, L0_conv_gamma2)
    x = x + _L1_conv_ref(_gn(x), L1_conv_kernel, L1_conv_bias, L1_conv_W)
    t = _to_tokens(x)
    t = t + _L2_attn_ref(_ln_t(t), L2_attn_Wq, L2_attn_bq, L2_attn_Wk, L2_attn_bk, L2_attn_Wv, L2_attn_bv)
    t = t + _L2_ffn_ref(_ln_t(t), L2_ffn_gate_w, L2_ffn_gate_b, L2_ffn_weight1, L2_ffn_weight2)
    t = t + _L3_attn_ref(_ln_t(t))
    t = t + _L3_ffn_ref(_ln_t(t), L3_ffn_router_w, L3_ffn_router_b, L3_ffn_expert_w, L3_ffn_expert_b)
    x = _from_tokens(t, x)
    return x


_drawn_inputs = setup_inputs


def setup_inputs(seed=0):
    import zlib

    import numpy as np

    out = dict(_drawn_inputs(seed))
    spreads = {'L0_conv_b_in': (0.0, 0.1),
     'L0_conv_dw_b': (0.0, 0.8),
     'L0_conv_bn_g': (1.0, 0.6),
     'L0_conv_bn_b': (0.0, 0.8),
     'L0_conv_b_off': (0.0, 0.412),
     'L0_conv_b_msk': (0.0, 0.8),
     'L0_conv_b_out': (0.0, 0.1),
     'L0_conv_ln1_g': (1.0, 0.2),
     'L0_conv_ln1_b': (0.0, 0.1),
     'L0_conv_b_fc1': (0.0, 0.1),
     'L0_conv_b_fc2': (0.0, 0.1),
     'L0_conv_ln2_g': (1.0, 0.2),
     'L0_conv_ln2_b': (0.0, 0.1),
     'L0_conv_gamma1': (1.0, 0.2),
     'L0_conv_gamma2': (1.0, 0.2),
     'L1_conv_bias': (0.0, 0.1),
     'L2_attn_bq': (0.0, 0.1),
     'L2_attn_bk': (0.0, 0.1),
     'L2_attn_bv': (0.0, 0.1),
     'L2_ffn_gate_b': (0.0, 0.1),
     'L3_ffn_router_b': (0.0, 2.0),
     'L3_ffn_expert_b': (0.0, 2.0)}
    factors = {'L0_conv_dw_w': 8.0,
     'L0_conv_bn_m': 8.0,
     'L0_conv_bn_v': 8.0,
     'L0_conv_w_off': 8.0,
     'L0_conv_w_msk': 8.0,
     'L2_ffn_gate_w': 64.0,
     'L2_ffn_weight1': 64.0,
     'L2_ffn_weight2': 64.0,
     'L3_ffn_router_w': 64.0,
     'L3_ffn_expert_w': 64.0}
    for name, (base, spread) in spreads.items():
        noise = np.random.default_rng([zlib.crc32(name.encode()), seed]).standard_normal(out[name].shape)
        drawn = base * np.exp(spread * noise) if base else spread * noise
        out[name] = jnp.asarray(drawn.astype(out[name].dtype))
    for name, factor in factors.items():
        out[name] = (out[name] * factor).astype(out[name].dtype)
    return out
```

```python
from contextlib import ExitStack

import concourse.bass as bass
from concourse import mybir

F32 = mybir.dt.float32
U32 = mybir.dt.uint32
BF16 = mybir.dt.bfloat16
ALU = mybir.AluOpType
ACT = mybir.ActivationFunctionType
AX = mybir.AxisListType
ds = bass.ds

N, H, W, C = 8, 56, 56, 128
HW = H * W
T = N * HW
P = 128
WP = W + 2
GROUPS, POINTS = 4, 9
GP = GROUPS * POINTS
CG = C // GROUPS
CORNER = (0, 1, WP, WP + 1)
POS_TILES = -(-((H + 1) * WP) // P)
POS = POS_TILES * P
XPAD = POS + WP + 2
STAGE = P + WP + 1
TILES = T // P
HID = 4 * C
MAGIC = 12582912.0


class Chain:

    def __init__(self, eng, sem, per):
        self.eng, self.sem, self.per, self.k, self.turn = eng, sem, per, 0, 0

    def begin(self, turn):
        assert self.k in (0, self.per), (self.k, self.per)
        self.turn, self.k = turn, 0

    def link(self, ins):
        ins.then_inc(self.sem, 1)
        self.k += 1
        self.eng.wait_ge(self.sem, self.turn * self.per + self.k)


def load_constants(nc, ctx, io, names, tag):
    tiles = {}
    for name in names:
        src = io[name]
        tiles[name] = ctx.enter_context(nc.sbuf_tensor(f"{tag}_{name}", list(src.shape), F32))
    s_const = ctx.enter_context(nc.semaphore(f"{tag}_consts_landed"))
    with nc.Block() as block:
        @block.sync
        def _(sp):
            for name in names:
                sp.dma_start(tiles[name][:], io[name]).then_inc(s_const, 16)
            sp.wait_ge(s_const, 16 * len(names))
    return tiles


def patches_and_features(nc, io, patch_table, feat_dram):
    with ExitStack() as ctx:
        def sb(name, shape, dt=F32):
            return ctx.enter_context(nc.sbuf_tensor(name, shape, dt))

        def sem(name):
            return ctx.enter_context(nc.semaphore(name))

        cst = load_constants(nc, ctx, io, ["w_in", "bias_in4", "interior4", "dw_w", "dw_b", "bn_g", "bn_b",
                                           "bn_m", "bn_v", "eps"], "p1")
        image = sb("image", [P, XPAD])
        conv = sb("conv", [P, H, W])
        feat = sb("feat", [P, HW])
        stage = sb("stage", [P, 2, STAGE])
        inside = sb("inside", [4, 2, P])
        patch = sb("patch", [P, 2, GROUPS, 4, CG])
        bn_scale = sb("bn_scale", [P, 1])
        bn_bias = sb("bn_bias", [P, 1])
        bn_std = sb("bn_std", [P, 1])
        ps = [ctx.enter_context(nc.psum_tensor(f"ps_patch{s}", [P, 4, C], F32)) for s in range(2)]

        image_landed = sem("image_landed")
        conv_done = sem("conv_done")
        conv_read = sem("conv_read")
        feat_stored = sem("feat_stored")
        staged = sem("staged")
        projected = sem("projected")
        patch_copied = sem("patch_copied")
        patch_stored = [sem(f"patch_stored{s}") for s in range(2)]
        dve_step = sem("p1_dve_step")
        bn_ready = sem("bn_ready")
        bn_root = sem("bn_root")
        HALF = POS_TILES // 2
        with nc.Block() as block:
            @block.sync
            def _(sp):
                with sp.Fori(0, N, 1) as n:
                    sp.wait_ge(conv_done, n + 1)
                    sp.dma_start(image[:], io["xT"][ds(n, 1)].rearrange("a p c -> (a p) c"))\
                        .then_inc(image_landed, 16)
                    with sp.Fori(0, HALF, 1) as i:
                        for s in range(2):
                            sp.wait_ge(patch_copied, n * POS_TILES + i * 2 + s + 1)
                            sp.dma_start(patch_table[ds(n * POS + (i * 2 + s) * P, P), :],
                                         patch[:, s].rearrange("p g k c -> p (g k c)"))\
                                .then_inc(patch_stored[s], 16)
                for s in range(2):
                    sp.wait_ge(patch_stored[s], 16 * N * HALF + 16)

            @block.scalar
            def _(act):
                nc.scalar.activation(bn_std[:], cst["bn_v"][:], ACT.Sqrt, bias=cst["eps"][:, 0:1])\
                    .then_inc(bn_root, 1)
                with act.Fori(0, N, 1) as n:
                    act.wait_ge(image_landed, 16 * (n + 1))
                    with act.Fori(0, HALF, 1) as i:
                        for s in range(2):
                            t = i * 2 + s
                            nc.scalar.copy(stage[:, s], image[:, ds(t * P, STAGE)]).then_inc(staged, 1)
                            nc.scalar.copy(inside[:, s], cst["interior4"][:, ds(t * P, P)]).then_inc(staged, 1)
                        for s in range(2):
                            act.wait_ge(projected, n * POS_TILES + i * 2 + s + 1)
                            act.wait_ge(patch_stored[s], (n * HALF + i) * 16 + 16)
                            nc.scalar.copy(patch[:, s].rearrange("p g k c -> p k g c"),
                                           ps[s][:].rearrange("p k (g c) -> p k g c", g=GROUPS))\
                                .then_inc(patch_copied, 1)
                    act.wait_ge(conv_done, n + 2)
                    act.wait_ge(bn_ready, 1)
                    act.wait_ge(feat_stored, 16 * n + 16)
                    nc.scalar.activation(feat[:], conv[:].rearrange("p h w -> p (h w)"), ACT.Gelu,
                                         bias=bn_bias[:, 0:1], scale=bn_scale[:, 0:1]).then_inc(conv_read, 1)
                    act.wait_ge(conv_read, n + 2)
                    act.dma_start(feat_dram[:, ds(n * HW, HW)], feat[:]).then_inc(feat_stored, 16)
                act.wait_ge(feat_stored, 16 * N + 16)

            @block.gpsimd
            def _(pool):
                pool.sem_inc(feat_stored, 16)
                pool.sem_inc(conv_read, 1)
                pool.sem_inc(conv_done, 1)
                for s in range(2):
                    pool.sem_inc(patch_stored[s], 16)

            @block.tensor
            def _(pe):
                with pe.Fori(0, N, 1) as n:
                    with pe.Fori(0, HALF, 1) as i:
                        for s in range(2):
                            pe.wait_ge(staged, 2 * (n * POS_TILES + i * 2 + s) + 2)
                            for k, step in enumerate(CORNER):
                                nc.tensor.matmul(ps[s][:, k, :], stage[:, s, step:step + P], cst["w_in"][:],
                                                 start=(k == 0), stop=False, skip_group_check=True)
                            nc.tensor.matmul(ps[s][:].rearrange("p k c -> p (k c)"), inside[:, s],
                                             cst["bias_in4"][:], start=False, stop=True, skip_group_check=True)\
                                .then_inc(projected, 1)

            @block.vector
            def _(dve):
                step = Chain(dve, dve_step, 4)
                step.begin(0)
                dve.wait_ge(bn_root, 1)
                step.link(nc.vector.reciprocal(bn_scale[:], bn_std[:]))
                step.link(nc.vector.tensor_tensor(bn_scale[:], bn_scale[:], cst["bn_g"][:], ALU.mult))
                step.link(nc.vector.tensor_tensor(bn_bias[:], cst["dw_b"][:], cst["bn_m"][:], ALU.subtract))
                step.link(nc.vector.tensor_tensor(bn_bias[:], bn_bias[:], bn_scale[:], ALU.mult))
                nc.vector.tensor_tensor(bn_bias[:], bn_bias[:], cst["bn_b"][:], ALU.add).then_inc(bn_ready, 1)
                rows = image[:, 0:WP * WP].rearrange("p (h w) -> p h w", w=WP)
                with dve.Fori(0, N, 1) as n:
                    dve.wait_ge(image_landed, 16 * (n + 1))
                    dve.wait_ge(conv_read, n + 1)
                    for k in range(9):
                        view = rows[:, k // 3:k // 3 + H, k % 3:k % 3 + W]
                        tap = cst["dw_w"][:, k:k + 1]
                        if k == 0:
                            ins = nc.vector.tensor_scalar(conv[:], view, tap, None, ALU.mult)
                        else:
                            ins = nc.vector.scalar_tensor_tensor(conv[:], view, tap, conv[:], ALU.mult, ALU.add)
                        if k < 8:
                            ins.then_inc(dve_step, 1)
                            dve.wait_ge(dve_step, 4 + n * 8 + k + 1)
                    ins.then_inc(conv_done, 1)


FRONT, BACK = 15, 13


def deformable_and_mlp(nc, io, patch_table, feat_dram, x2_dram):
    with ExitStack() as ctx:
        def sb(name, shape, dt=F32):
            return ctx.enter_context(nc.sbuf_tensor(name, shape, dt))

        def sem(name):
            return ctx.enter_context(nc.semaphore(name))

        cst = load_constants(nc, ctx, io, ["w_om", "b_om", "grid", "tok_base", "row_base", "group_col", "w_out",
                                           "b_out", "ln1_g", "ln1_b", "gamma1", "w_fc1", "b_fc1", "w_fc2",
                                           "b_fc2", "ln2_g", "ln2_b", "gamma2", "ident", "eps"], "p2")
        featT = sb("featT", [P, 2, P])
        xin = sb("xin", [P, 2, C])
        om = sb("om", [P, 3 * GP])
        u = sb("u", [P, GP, 2])
        fl = sb("fl", [P, GP, 2])
        fr = sb("fr", [P, GP, 2])
        lin = sb("lin", [P, GP])
        idx = sb("idx", [P, 2, GP], U32)
        mx = sb("mx", [P, GROUPS])
        lg = sb("lg", [P, GROUPS, POINTS])
        ex = sb("ex", [P, GROUPS, POINTS])
        ssum = sb("ssum", [P, GROUPS])
        msk = sb("msk", [P, GP])
        lo = sb("lo", [P, GP])
        hi = sb("hi", [P, GP])
        wts = sb("wts", [P, 2, GP, 4])
        got = sb("got", [P, 2, GP, 4 * CG])
        samp = sb("samp", [P, C])
        sampT = sb("sampT", [P, P])
        y = sb("y", [P, C])
        st = sb("st", [P, 6])
        mv = sb("mv", [P, 2])
        rs = sb("rs", [P, 1])
        x1 = sb("x1", [P, C])
        x1T = sb("x1T", [P, P])
        hT = sb("hT", [P, 4, P])
        x2 = sb("x2", [P, 2, C])
        g1 = sb("g1", [P, C])
        b1 = sb("b1", [P, C])
        g2 = sb("g2", [P, C])
        b2 = sb("b2", [P, C])

        def pb(name, n):
            return ctx.enter_context(nc.psum_tensor(name, [P, n], F32))
        ps_om = [pb(f"ps_om{s}", 512) for s in range(2)]
        ps_t = pb("ps_t", 512)
        ps_y = pb("ps_y", 512)
        ps_h = pb("ps_h", 512)
        ps_m = pb("ps_m", 512)

        feat_landed = [sem(f"feat_landed{s}") for s in range(2)]
        x_landed = [sem(f"x_landed{s}") for s in range(2)]
        om_ready = sem("om_ready")
        om_read = sem("om_read")
        logits_ready = sem("logits_ready")
        exp_ready = sem("exp_ready")
        idx_ready = sem("idx_ready")
        weights_ready = sem("weights_ready")
        gathered = [sem(f"gathered{s}") for s in range(2)]
        gather_begun = sem("gather_begun")
        sampled = sem("sampled")
        samp_turned = sem("samp_turned")
        sampT_ready = sem("sampT_ready")
        y_ready = sem("y_ready")
        x1_ready = sem("x1_ready")
        x1_turned = sem("x1_turned")
        x1T_ready = sem("x1T_ready")
        h_ready = sem("h_ready")
        hT_ready = sem("hT_ready")
        m_ready = sem("m_ready")
        stats_turn = sem("stats_turn")
        var_ready = sem("var_ready")
        std_ready = sem("std_ready")
        x2_ready = sem("x2_ready")
        x2_stored = [sem(f"x2_stored{s}") for s in range(2)]
        front_step = sem("front_step")
        back_step = sem("back_step")
        setup_step = sem("setup_step")

        xf = io["x"]
        with nc.Block() as block:
            @block.sync
            def _(sp):
                def load(t, s):
                    sp.dma_start(featT[:, s], feat_dram[:, ds(t * P, P)]).then_inc(feat_landed[s], 16)
                    sp.dma_start(xin[:, s], xf[ds(t * P, P), :]).then_inc(x_landed[s], 16)

                def store(t, s):
                    sp.wait_ge(x2_ready, t + 1)
                    sp.dma_start(x2_dram[ds(t * P, P), :], x2[:, s]).then_inc(x2_stored[s], 16)
                for s in range(2):
                    load(s, s)
                with sp.Fori(0, TILES // 2 - 1, 1) as i:
                    for s in range(2):
                        store(2 * i + s, s)
                        load(2 * i + s + 2, s)
                for s in range(2):
                    store(TILES - 2 + s, s)
                for s in range(2):
                    sp.wait_ge(x2_stored[s], 16 * (TILES // 2) + 16)

            @block.gpsimd
            def _(pool):
                for s in range(2):
                    pool.sem_inc(x2_stored[s], 16)

                def gather(t, s, primed):
                    pool.wait_ge(idx_ready, t + 1)
                    if not primed:
                        pool.wait_ge(sampled, t - 1)
                        pool.sem_inc(gather_begun, 1)
                    for k in range(GP):
                        pool.indirect_dma_start(got[:, s, k], None, patch_table.rearrange("r (g c) -> (r g) c", g=GROUPS),
                                                bass.IndirectOffsetOnAxis(ap=idx[:, s, k:k + 1], axis=0))\
                            .then_inc(gathered[s], 16)
                for s in range(2):
                    gather(s, s, True)
                with pool.Fori(1, TILES // 2, 1) as i:
                    for s in range(2):
                        gather(2 * i + s, s, False)

            @block.tensor
            def _(pe):
                def front(t, s, primed=False):
                    pe.wait_ge(feat_landed[s], (t - s) * 8 + 16)
                    if not primed:
                        pe.wait_ge(om_read, t - 1)
                    nc.tensor.matmul(ps_om[s][:, 0:3 * GP], featT[:, s], cst["w_om"][:], start=True, stop=True)\
                        .then_inc(om_ready, 1)

                def back(t, s):
                    pe.wait_ge(sampled, t + 1)
                    nc.tensor.transpose(ps_t[:, 0:P], samp[:], cst["ident"][:]).then_inc(samp_turned, 1)
                    pe.wait_ge(sampT_ready, t + 1)
                    nc.tensor.matmul(ps_y[:, 0:C], sampT[:], cst["w_out"][:], start=True, stop=True)\
                        .then_inc(y_ready, 1)
                    pe.wait_ge(x1_ready, t + 1)
                    nc.tensor.transpose(ps_t[:, 0:P], x1[:], cst["ident"][:]).then_inc(x1_turned, 1)
                    pe.wait_ge(x1T_ready, t + 1)
                    for j in range(4):
                        mm = nc.tensor.matmul(ps_h[:, j * P:(j + 1) * P], cst["w_fc1"][:, j * P:(j + 1) * P], x1T[:],
                                              start=True, stop=True)
                    mm.then_inc(h_ready, 1)
                    pe.wait_ge(hT_ready, t + 1)
                    for j in range(4):
                        mm = nc.tensor.matmul(ps_m[:, 0:C], hT[:, j], cst["w_fc2"][:, j * C:(j + 1) * C],
                                              start=(j == 0), stop=(j == 3))
                    mm.then_inc(m_ready, 1)
                front(0, 0, True)
                front(1, 1, True)
                back(0, 0)
                with pe.Fori(0, TILES // 2 - 1, 1) as i:
                    front(2 * i + 2, 0)
                    back(2 * i + 1, 1)
                    front(2 * i + 3, 1)
                    back(2 * i + 2, 0)
                back(TILES - 1, 1)

            @block.scalar
            def _(act):
                def front(t):
                    act.wait_ge(logits_ready, t + 1)
                    nc.scalar.activation(ex[:], lg[:], ACT.Exp).then_inc(exp_ready, 1)

                def root(nth):
                    act.wait_ge(var_ready, nth)
                    nc.scalar.activation(rs[:], mv[:, 1:2], ACT.Sqrt, bias=cst["eps"][:, 0:1]).then_inc(std_ready, 1)

                def back(t):
                    act.wait_ge(samp_turned, t + 1)
                    nc.scalar.copy(sampT[:], ps_t[:, 0:P]).then_inc(sampT_ready, 1)
                    root(2 * t + 1)
                    act.wait_ge(x1_turned, t + 1)
                    nc.scalar.copy(x1T[:], ps_t[:, 0:P]).then_inc(x1T_ready, 1)
                    act.wait_ge(h_ready, t + 1)
                    for j in range(4):
                        g = nc.scalar.activation(hT[:, j], ps_h[:, j * P:(j + 1) * P], ACT.Gelu,
                                                 bias=cst["b_fc1"][:, j:j + 1])
                    g.then_inc(hT_ready, 1)
                    root(2 * t + 2)
                front(0)
                front(1)
                back(0)
                with act.Fori(0, TILES // 2 - 1, 1) as i:
                    front(2 * i + 2)
                    back(2 * i + 1)
                    front(2 * i + 3)
                    back(2 * i + 2)
                back(TILES - 1)

            @block.vector
            def _(dve):
                V = nc.vector
                fc = Chain(dve, front_step, FRONT)
                bc = Chain(dve, back_step, BACK)
                sc = Chain(dve, setup_step, 5)
                sc.begin(0)
                sc.link(V.tensor_tensor(g1[:], cst["ln1_g"][:], cst["gamma1"][:], ALU.mult))
                sc.link(V.tensor_tensor(b1[:], cst["ln1_b"][:], cst["gamma1"][:], ALU.mult))
                sc.link(V.tensor_tensor(g2[:], cst["ln2_g"][:], cst["gamma2"][:], ALU.mult))
                sc.link(V.tensor_tensor(b2[:], cst["ln2_b"][:], cst["gamma2"][:], ALU.mult))
                sc.link(V.tensor_tensor(cst["b_om"][:], cst["b_om"][:], cst["grid"][:], ALU.add))

                def front(t, s):
                    fc.begin(t)
                    dve.wait_ge(om_ready, t + 1)
                    V.tensor_tensor(om[:], ps_om[s][:, 0:3 * GP], cst["b_om"][:], ALU.add).then_inc(om_read, 1)
                    dve.wait_ge(om_read, t + 1)
                    logits = om[:, 2 * GP:3 * GP].rearrange("p (g k) -> p g k", g=GROUPS)
                    fc.link(V.tensor_reduce(mx[:], logits, AX.X, ALU.max))
                    V.tensor_tensor(lg[:], logits, mx[:].unsqueeze(2).to_broadcast([P, GROUPS, POINTS]),
                                    ALU.subtract).then_inc(logits_ready, 1)
                    base = cst["tok_base"][:, ds(t * 2, 2)].unsqueeze(1).to_broadcast([P, GP, 2])
                    fc.link(V.tensor_tensor(u[:], om[:, 0:2 * GP].rearrange("p (k c) -> p k c", c=2), base, ALU.add))
                    fc.link(V.tensor_scalar(u[:], u[:], -0.5, H + 0.5, ALU.max, ALU.min))
                    fc.link(V.tensor_scalar(fl[:], u[:], MAGIC, None, ALU.add))
                    fc.link(V.tensor_scalar(fl[:], fl[:], MAGIC, None, ALU.subtract))
                    fc.link(V.scalar_tensor_tensor(fr[:], u[:], 0.5, fl[:], ALU.add, ALU.subtract))
                    fc.link(V.scalar_tensor_tensor(lin[:], fl[:, :, 1], float(WP), fl[:, :, 0], ALU.mult, ALU.add))
                    fc.link(V.tensor_scalar(lin[:], lin[:], float(GROUPS), cst["row_base"][:, ds(t, 1)],
                                            ALU.mult, ALU.add))
                    V.tensor_tensor(idx[:, s], lin[:], cst["group_col"][:], ALU.add).then_inc(idx_ready, 1)
                    dve.wait_ge(exp_ready, t + 1)
                    fc.link(V.tensor_reduce(ssum[:], ex[:], AX.X, ALU.add))
                    fc.link(V.reciprocal(ssum[:], ssum[:]))
                    fc.link(V.tensor_tensor(msk[:].rearrange("p (g k) -> p g k", g=GROUPS), ex[:],
                                            ssum[:].unsqueeze(2).to_broadcast([P, GROUPS, POINTS]), ALU.mult))
                    fc.link(V.tensor_tensor(lo[:], msk[:], fr[:, :, 1], ALU.mult))
                    fc.link(V.tensor_tensor(hi[:], msk[:], lo[:], ALU.subtract))
                    fc.link(V.tensor_tensor(wts[:, s, :, 3], lo[:], fr[:, :, 0], ALU.mult))
                    fc.link(V.tensor_tensor(wts[:, s, :, 1], hi[:], fr[:, :, 0], ALU.mult))
                    V.tensor_tensor(wts[:, s, :, 2], lo[:], wts[:, s, :, 3], ALU.subtract).then_inc(weights_ready, 1)
                    V.tensor_tensor(wts[:, s, :, 0], hi[:], wts[:, s, :, 1], ALU.subtract).then_inc(weights_ready, 1)

                def norm(g, b, res, out, nth, ready):
                    bc.link(V.bn_stats(st[:], y[:]))
                    dve.sem_inc(stats_turn, 1)
                    V.bn_aggr(mv[:], st[:]).then_inc(var_ready, 1)
                    dve.wait_ge(std_ready, nth)
                    bc.link(V.reciprocal(rs[:], rs[:]))
                    bc.link(V.tensor_scalar(y[:], y[:], mv[:, 0:1], rs[:, 0:1], ALU.subtract, ALU.mult))
                    bc.link(V.tensor_tensor(y[:], y[:], g[:], ALU.mult))
                    bc.link(V.tensor_tensor(y[:], y[:], b[:], ALU.add))
                    V.tensor_tensor(out, y[:], res, ALU.add).then_inc(ready, 1)

                def back(t, s):
                    bc.begin(t)
                    dve.wait_ge(gathered[s], (t - s) * (8 * GP) + 16 * GP)
                    dve.wait_ge(weights_ready, 2 * t + 2)
                    v = got[:, s].rearrange("p k (q c) -> p (k q) c", q=4)
                    w = wts[:, s].rearrange("p k q -> p (k q)").unsqueeze(2).to_broadcast([P, GP * 4, CG])
                    bc.link(V.tensor_tensor(v, v, w, ALU.mult))
                    V.tensor_reduce(samp[:].rearrange("p (g c) -> p g c", g=GROUPS),
                                    got[:, s].rearrange("p (g k) (q c) -> p g c (k q)", g=GROUPS, q=4),
                                    AX.X, ALU.add).then_inc(sampled, 1)
                    dve.wait_ge(y_ready, t + 1)
                    dve.wait_ge(x_landed[s], (t - s) * 8 + 16)
                    bc.link(V.tensor_tensor(y[:], ps_y[:, 0:C], cst["b_out"][:], ALU.add))
                    norm(g1, b1, xin[:, s], x1[:], 2 * t + 1, x1_ready)
                    dve.wait_ge(m_ready, t + 1)
                    dve.wait_ge(x1_ready, t + 1)
                    dve.wait_ge(x2_stored[s], (t - s) * 8 + 16)
                    bc.link(V.tensor_tensor(y[:], ps_m[:, 0:C], cst["b_fc2"][:], ALU.add))
                    norm(g2, b2, x1[:], x2[:, s], 2 * t + 2, x2_ready)
                front(0, 0)
                front(1, 1)
                back(0, 0)
                with dve.Fori(0, TILES // 2 - 1, 1) as i:
                    front(2 * i + 2, 0)
                    back(2 * i + 1, 1)
                    front(2 * i + 3, 1)
                    back(2 * i + 2, 0)
                back(TILES - 1, 1)


TT = 2 * W
IT = HW // TT
CH = 4
CHUNKS = IT // CH
CT = CH * TT
CROWS = CT // W
EXPERTS, TOPK = 64, 8
ROUTED = 8
P3_LINKS, P5_LINKS = 51, 343


class Turns:

    def __init__(self, sem, per):
        self.sem, self.per = sem, per

    def wait(self, eng, n, k):
        eng.wait_ge(self.sem, n * self.per + k)


def image_view(dram, n):
    return dram[ds(n * HW, HW), :].rearrange("(a p) c -> p a c", p=TT)


def norm_conv_attention_gate(nc, io, pooledT, x2_dram, t1_dram, sel_dram):
    with ExitStack() as ctx:
        def sb(name, shape, dt=F32):
            return ctx.enter_context(nc.sbuf_tensor(name, shape, dt))

        cst = load_constants(nc, ctx, io, ["kernelT", "conv_bias", "W", "group_avg", "Wq", "bq", "Wk", "bk", "Wv",
                                           "bv", "gate_wT", "gate_b", "ident", "eps"], "p3")
        fused = sb("fused", [P, 9, C])
        fused_bias = sb("fused_bias", [P, 1])
        xt = sb("xt", [TT, IT, C])
        gimg = sb("gimg", [P, WP * WP])
        grows = gimg[:].rearrange("p (h w) -> p h w", w=WP)
        cstat = sb("cstat", [P, CHUNKS, 6])
        cmv = sb("cmv", [P, 2])
        gmean = sb("gmean", [P, 1])
        dev = sb("dev", [P, 1])
        spread = sb("spread", [P, 1])
        gstd = sb("gstd", [P, 1])
        cT = sb("cT", [P, 2, CT])
        st = sb("st3", [TT, CH, 6])
        mv = sb("mv3", [TT, CH, 2])
        rs = sb("rs3", [TT, CH])
        un = sb("un", [TT, 2, CH, C])
        uT = sb("uT", [P, CHUNKS, CT])
        ksb = sb("ksb", [P, CT])
        kv_junk = sb("kv_junk", [P, CT])
        kvp = sb("kvp", [P, CHUNKS])
        kv = sb("kv", [P, 1])
        bqkv = sb("bqkv", [P, 1])
        u2 = sb("u2", [TT, IT, C])
        u2T = sb("u2T", [P, 2, CT])
        lg = sb("lg3", [EXPERTS, HW])
        pr = sb("pr3", [EXPERTS, HW])
        rep = sb("rep3", [EXPERTS, HW])
        nmx = sb("nmx", [EXPERTS, 1])
        psum_e = sb("psum_e", [EXPERTS, 1])
        top = sb("top", [EXPERTS, 8])
        selT = sb("selT", [TT, 2, CH, EXPERTS])
        pooled = sb("pooled", [EXPERTS, C])
        bank = [ctx.enter_context(nc.psum_tensor(f"bank{k}", [P, 512], F32)) for k in range(8)]

        def sem(name, per=CHUNKS):
            return Turns(ctx.enter_context(nc.semaphore(name)), per)
        fuse_ready, fuse_copied, border_zeroed = sem("fuse_ready"), sem("fuse_copied"), sem("border_zeroed")
        image_done = sem("image_done", 1)
        x_landed = sem("x2_landed", 16)
        t1_stored = sem("t1_stored", 16)
        sel_stored = sem("sel_stored", 16)
        turned = sem("x2_turned")
        gimg_copied = sem("gimg_copied")
        stats_taken = sem("stats_taken")
        mean_ready = sem("mean_ready", 1)
        gmean_ready = sem("gmean_ready", 1)
        spread_ready = sem("spread_ready", 1)
        gvar_ready = sem("gvar_ready", 1)
        gstd_ready = sem("gstd_ready", 1)
        normed = sem("normed", 1)
        conv_ready = sem("conv_ready")
        cT_ready = sem("cT_ready")
        c_turned = sem("c_turned")
        var_ready = sem("var3_ready", 2 * CHUNKS)
        std_ready = sem("std3_ready", 2 * CHUNKS)
        u_ready = sem("u_ready")
        u_turned = sem("u_turned")
        uT_ready = sem("uT_ready")
        k_ready = sem("k_ready")
        v_ready = sem("v_ready")
        ksb_ready = sem("ksb_ready")
        kv_summed = sem("kv_summed")
        kv_ready = sem("kv_ready", 1)
        q_ready = sem("q_ready")
        qT_ready = sem("qT_ready")
        q_turned = sem("q_turned")
        u2_ready = sem("u2_ready")
        u2_turned = sem("u2_turned")
        u2T_ready = sem("u2T_ready")
        gate_ready = sem("gate_ready")
        lg_ready = sem("lg_ready")
        max_ready = sem("max_ready", 1)
        prob_ready = sem("prob_ready", 1)
        sel_ready = sem("sel_ready", 1)
        sel_turned = sem("sel_turned")
        selT_ready = sem("selT_ready")
        pool_step = sem("pool_step")
        pooled_copied = sem("pooled_copied", 1)
        pooled_turned = sem("pooled_turned", 1)
        chain = ctx.enter_context(nc.semaphore("dve3_step"))
        tick = ctx.enter_context(nc.semaphore("dve3_tick"))
        pe_tick = ctx.enter_context(nc.semaphore("pe3_tick"))
        sp_tick = ctx.enter_context(nc.semaphore("sp3_tick"))

        with nc.Block() as block:
            @block.sync
            def _(sp):
                with sp.Fori(0, N, 1) as n:
                    image_done.wait(sp, n, 1)
                    sp.sem_inc(sp_tick, 1)
                    sp.dma_start(xt[:], image_view(x2_dram, n)).then_inc(x_landed.sem, 16)
                    u2_ready.wait(sp, n, CHUNKS)
                    sp.sem_inc(sp_tick, 1)
                    sp.dma_start(image_view(t1_dram, n), xt[:]).then_inc(t1_stored.sem, 16)
                    sel_ready.wait(sp, n, 1)
                    sp.sem_inc(sp_tick, 1)
                    sp.dma_start(sel_dram[ds(n * EXPERTS, EXPERTS), :], pr[:]).then_inc(sel_stored.sem, 16)
                    t1_stored.wait(sp, n, 16)
                    sel_stored.wait(sp, n, 16)
                    sp.sem_inc(sp_tick, 1)

            @block.gpsimd
            def _(pool):
                pool.sem_inc(image_done.sem, 1)
                pool.memset(gimg[:], 0.0).then_inc(border_zeroed.sem, 1)

            @block.tensor
            def _(pe):
                for k in range(9):
                    nc.tensor.matmul(bank[k // 4][:, (k % 4) * C:(k % 4 + 1) * C], cst["kernelT"][:, k * C:(k + 1) * C],
                                     cst["W"][:], start=True, stop=True)
                nc.tensor.matmul(bank[3][:, 0:1], cst["W"][:], cst["conv_bias"][:], start=True, stop=True)\
                    .then_inc(fuse_ready.sem, 1)
                pe.wait_ge(fuse_copied.sem, 4)

                def turn(dst, src, parts):
                    for a in range(CH):
                        ins = nc.tensor.transpose(dst(a), src(a), cst["ident"][0:parts, 0:parts])
                    return ins

                def cols(b, a, rows=P):
                    return bank[b][0:rows, a * TT:(a + 1) * TT]

                with pe.Fori(0, N, 1) as n:
                    x_landed.wait(pe, n, 16)
                    for j in range(CHUNKS):
                        if j >= 2:
                            gimg_copied.wait(pe, n, j - 1)
                        turn(lambda a: cols(j % 2, a), lambda a: xt[:, j * CH + a, :], TT).then_inc(turned.sem, 1)
                    mean_ready.wait(pe, n, 1)
                    nc.tensor.matmul(bank[2][:, 0:1], cst["group_avg"][:], cmv[:, 0:1], start=True, stop=True)\
                        .then_inc(gmean_ready.sem, 1)
                    spread_ready.wait(pe, n, 1)
                    nc.tensor.matmul(bank[3][:, 0:1], cst["group_avg"][:], spread[:], start=True, stop=True)\
                        .then_inc(gvar_ready.sem, 1)
                    normed.wait(pe, n, 1)

                    def conv(j):
                        for k in range(9):
                            r = j * CROWS + k // 3
                            mm = nc.tensor.matmul(bank[j % 2][:, 0:CT], fused[:, k, :],
                                                  grows[:, r:r + CROWS, k % 3:k % 3 + W],
                                                  start=(k == 0), stop=(k == 8))
                        mm.then_inc(conv_ready.sem, 1)
                    conv(0)
                    for j in range(CHUNKS):
                        cT_ready.wait(pe, n, j + 1)
                        turn(lambda a: bank[2][0:TT, a * C:(a + 1) * C], lambda a: cT[:, j % 2, a * TT:(a + 1) * TT], P)\
                            .then_inc(c_turned.sem, 1)
                        if j + 1 < CHUNKS:
                            conv(j + 1)
                        u_ready.wait(pe, n, j + 1)
                        turn(lambda a: cols(3, a), lambda a: un[:, j % 2, a, :], TT).then_inc(u_turned.sem, 1)
                        uT_ready.wait(pe, n, j + 1)
                        if j:
                            kv_summed.wait(pe, n, j)
                        nc.tensor.matmul(bank[4][:, 0:CT], cst["Wk"][:], uT[:, j], start=True, stop=True)\
                            .then_inc(k_ready.sem, 1)
                        nc.tensor.matmul(bank[5][:, 0:CT], cst["Wv"][:], uT[:, j], start=True, stop=True)\
                            .then_inc(v_ready.sem, 1)

                    def query(j):
                        nc.tensor.matmul(bank[j % 2][:, 0:CT], cst["Wq"][:], uT[:, j], start=True, stop=True)\
                            .then_inc(q_ready.sem, 1)
                    query(0)
                    kv_summed.wait(pe, n, CHUNKS)
                    for j in range(CHUNKS):
                        qT_ready.wait(pe, n, j + 1)
                        turn(lambda a: bank[2][0:TT, a * C:(a + 1) * C], lambda a: cT[:, j % 2, a * TT:(a + 1) * TT], P)\
                            .then_inc(q_turned.sem, 1)
                        if j + 1 < CHUNKS:
                            query(j + 1)
                        u2_ready.wait(pe, n, j + 1)
                        turn(lambda a: cols(3, a), lambda a: u2[:, j * CH + a, :], TT).then_inc(u2_turned.sem, 1)
                        u2T_ready.wait(pe, n, j + 1)
                        if j:
                            lg_ready.wait(pe, n, j)
                        nc.tensor.matmul(bank[4][0:EXPERTS, 0:CT], cst["gate_wT"][:], u2T[:, j % 2],
                                         start=True, stop=True).then_inc(gate_ready.sem, 1)
                    sel_ready.wait(pe, n, 1)

                    pe.sem_inc(pe_tick, 1)

                    def turn_sel(j):
                        turn(lambda a: bank[j % 2][0:TT, a * EXPERTS:(a + 1) * EXPERTS],
                             lambda a: pr[:, (j * CH + a) * TT:(j * CH + a + 1) * TT], EXPERTS)\
                            .then_inc(sel_turned.sem, 1)
                    turn_sel(0)
                    for j in range(CHUNKS):
                        if j + 1 < CHUNKS:
                            turn_sel(j + 1)
                        selT_ready.wait(pe, n, j + 1)
                        for a in range(CH):
                            mm = nc.tensor.matmul(bank[5][0:EXPERTS, 0:C], selT[:, j % 2, a], u2[:, j * CH + a, :],
                                                  start=(j == 0 and a == 0), stop=(j == CHUNKS - 1 and a == CH - 1))
                        mm.then_inc(pool_step.sem, 1)
                    pooled_copied.wait(pe, n, 1)
                    pe.sem_inc(pe_tick, 1)
                    nc.tensor.transpose(bank[6][:, 0:EXPERTS], pooled[:], cst["ident"][0:EXPERTS, 0:EXPERTS])\
                        .then_inc(pooled_turned.sem, 1)

            @block.scalar
            def _(act):
                S = nc.scalar
                act.wait_ge(fuse_ready.sem, 1)
                for k in range(2):
                    S.copy(fused[:, 4 * k:4 * k + 4].rearrange("p k c -> p (k c)"), bank[k][:]).then_inc(fuse_copied.sem, 1)
                S.copy(fused[:, 8], bank[2][:, 0:C]).then_inc(fuse_copied.sem, 1)
                S.copy(fused_bias[:], bank[3][:, 0:1]).then_inc(fuse_copied.sem, 1)
                act.wait_ge(fuse_copied.sem, 4)
                act.wait_ge(border_zeroed.sem, 1)
                with act.Fori(0, N, 1) as n:
                    for j in range(CHUNKS):
                        turned.wait(act, n, j + 1)
                        S.copy(grows[:, 1 + j * CROWS:1 + (j + 1) * CROWS, 1:1 + W],
                               bank[j % 2][:, 0:CT].rearrange("p (h w) -> p h w", w=W)).then_inc(gimg_copied.sem, 1)
                    gvar_ready.wait(act, n, 1)
                    S.activation(gstd[:], bank[3][:, 0:1], ACT.Sqrt, bias=cst["eps"][:, 0:1]).then_inc(gstd_ready.sem, 1)

                    def root(k):
                        var_ready.wait(act, n, k)
                        S.activation(rs[:], mv[:, :, 1], ACT.Sqrt, bias=cst["eps"][0:TT, 0:1]).then_inc(std_ready.sem, 1)

                    def conv_out(j):
                        conv_ready.wait(act, n, j + 1)
                        S.activation(cT[:, j % 2], bank[j % 2][:, 0:CT], ACT.Identity, bias=fused_bias[:, 0:1])\
                            .then_inc(cT_ready.sem, 1)
                    conv_out(0)
                    for j in range(CHUNKS):
                        root(j + 1)
                        if j + 1 < CHUNKS:
                            conv_out(j + 1)
                        u_turned.wait(act, n, j + 1)
                        S.copy(uT[:, j], bank[3][:, 0:CT]).then_inc(uT_ready.sem, 1)
                        k_ready.wait(act, n, j + 1)
                        if j:
                            kv_summed.wait(act, n, j)
                        S.activation(ksb[:], bank[4][:, 0:CT], ACT.Identity, bias=cst["bk"][:, 0:1])\
                            .then_inc(ksb_ready.sem, 1)
                    kv_ready.wait(act, n, 1)

                    def query_out(j):
                        q_ready.wait(act, n, j + 1)
                        S.activation(cT[:, j % 2], bank[j % 2][:, 0:CT], ACT.Identity, bias=bqkv[:, 0:1],
                                     scale=kv[:, 0:1]).then_inc(qT_ready.sem, 1)
                    query_out(0)
                    for j in range(CHUNKS):
                        root(CHUNKS + j + 1)
                        if j + 1 < CHUNKS:
                            query_out(j + 1)
                        u2_turned.wait(act, n, j + 1)
                        S.copy(u2T[:, j % 2], bank[3][:, 0:CT]).then_inc(u2T_ready.sem, 1)
                        gate_ready.wait(act, n, j + 1)
                        S.activation(lg[:, j * CT:(j + 1) * CT], bank[4][0:EXPERTS, 0:CT], ACT.Identity,
                                     bias=cst["gate_b"][:, 0:1]).then_inc(lg_ready.sem, 1)
                    max_ready.wait(act, n, 1)
                    S.activation(lg[:], lg[:], ACT.Exp, bias=nmx[:, 0:1], accum_out=psum_e[:, 0:1])\
                        .then_inc(prob_ready.sem, 1)
                    for j in range(CHUNKS):
                        sel_turned.wait(act, n, j + 1)
                        if j >= 2:
                            pool_step.wait(act, n, j - 1)
                        S.copy(selT[:, j % 2].rearrange("p a e -> p (a e)"), bank[j % 2][0:TT, 0:CH * EXPERTS])\
                            .then_inc(selT_ready.sem, 1)
                    pool_step.wait(act, n, CHUNKS)
                    S.copy(pooled[:], bank[5][0:EXPERTS, 0:C]).then_inc(pooled_copied.sem, 1)
                    pooled_turned.wait(act, n, 1)
                    S.copy(pooledT[:, ds(n, 1), :].rearrange("p n e -> p (n e)"), bank[6][:, 0:EXPERTS])\
                        .then_inc(image_done.sem, 1)

            @block.vector
            def _(dve):
                V = nc.vector
                cc = Chain(dve, chain, 0)
                with dve.Fori(0, N, 1) as n:
                    cc.turn, cc.per, cc.k = n, P3_LINKS, 0
                    for j in range(CHUNKS):
                        gimg_copied.wait(dve, n, j + 1)
                        V.bn_stats(cstat[:, j], grows[:, 1 + j * CROWS:1 + (j + 1) * CROWS, 1:1 + W])\
                            .then_inc(stats_taken.sem, 1)
                    stats_taken.wait(dve, n, CHUNKS)
                    dve.sem_inc(tick, 1)
                    V.bn_aggr(cmv[:], cstat[:].rearrange("p j k -> p (j k)")).then_inc(mean_ready.sem, 1)
                    gmean_ready.wait(dve, n, 1)
                    cc.link(V.tensor_copy(gmean[:], bank[2][:, 0:1]))
                    cc.link(V.tensor_tensor(dev[:], cmv[:, 0:1], gmean[:], ALU.subtract))
                    V.scalar_tensor_tensor(spread[:], dev[:], dev[:, 0:1], cmv[:, 1:2], ALU.mult, ALU.add)\
                        .then_inc(spread_ready.sem, 1)
                    gstd_ready.wait(dve, n, 1)
                    gimg_copied.wait(dve, n, CHUNKS)
                    cc.link(V.reciprocal(gstd[:], gstd[:]))
                    inner = grows[:, 1:1 + H, 1:1 + W]
                    V.tensor_scalar(inner, inner, gmean[:, 0:1], gstd[:, 0:1], ALU.subtract, ALU.mult)\
                        .then_inc(normed.sem, 1)

                    def add_and_norm(j, out, k, ready):
                        x = xt[:, j * CH:(j + 1) * CH, :]
                        cc.link(V.tensor_tensor(x, x, bank[2][0:TT, 0:CH * C].rearrange("p (a c) -> p a c", a=CH), ALU.add))
                        for a in range(CH):
                            ins = V.bn_stats(st[:, a], xt[:, j * CH + a, :])
                        cc.link(ins)
                        dve.sem_inc(tick, 1)
                        for a in range(CH):
                            ins = V.bn_aggr(mv[:, a], st[:, a])
                        ins.then_inc(var_ready.sem, 1)
                        std_ready.wait(dve, n, k)
                        cc.link(V.reciprocal(rs[:], rs[:]))
                        for a in range(CH):
                            ins = V.tensor_scalar(out(a), xt[:, j * CH + a, :], mv[:, a, 0:1], rs[:, a:a + 1],
                                                  ALU.subtract, ALU.mult)
                        ins.then_inc(ready.sem, 1)

                    for j in range(CHUNKS):
                        c_turned.wait(dve, n, j + 1)
                        add_and_norm(j, lambda a: un[:, j % 2, a, :], j + 1, u_ready)
                        v_ready.wait(dve, n, j + 1)
                        ksb_ready.wait(dve, n, j + 1)
                        V.scalar_tensor_tensor(kv_junk[:], bank[5][:, 0:CT], cst["bv"][:, 0:1], ksb[:], ALU.add,
                                               ALU.mult, accum_out=kvp[:, j:j + 1]).then_inc(kv_summed.sem, 1)
                    kv_summed.wait(dve, n, CHUNKS)
                    cc.link(V.tensor_reduce(kv[:], kvp[:], AX.X, ALU.add))
                    V.tensor_tensor(bqkv[:], cst["bq"][:], kv[:], ALU.mult).then_inc(kv_ready.sem, 1)
                    for j in range(CHUNKS):
                        q_turned.wait(dve, n, j + 1)
                        add_and_norm(j, lambda a: u2[:, j * CH + a, :], CHUNKS + j + 1, u2_ready)
                    lg_ready.wait(dve, n, CHUNKS)
                    cc.link(V.tensor_reduce(nmx[:], lg[:], AX.X, ALU.max))
                    V.tensor_scalar(nmx[:], nmx[:], -1.0, None, ALU.mult).then_inc(max_ready.sem, 1)
                    prob_ready.wait(dve, n, 1)
                    dve.sem_inc(tick, 1)
                    cc.link(V.max(top[:], lg[:]))
                    dve.sem_inc(tick, 1)
                    cc.link(V.match_replace(rep[:], top[:], lg[:], 0.0))
                    cc.link(V.reciprocal(psum_e[:], psum_e[:]))
                    cc.link(V.tensor_tensor(rep[:], lg[:], rep[:], ALU.subtract))
                    V.tensor_scalar(pr[:], rep[:], psum_e[:, 0:1], None, ALU.mult).then_inc(sel_ready.sem, 1)
                    assert cc.k == P3_LINKS, cc.k


def pooled_experts(nc, io, pooledT, outE_dram):
    SLOTS = 4
    with ExitStack() as ctx:
        def sb(name, shape, dt=F32):
            return ctx.enter_context(nc.sbuf_tensor(name, shape, dt))

        cst = load_constants(nc, ctx, io, ["e_b1", "e_b2"], "p4")
        w1 = sb("w1", [P, SLOTS, HID])
        w2 = sb("w2", [P, SLOTS, 4 * C])
        h = sb("h4", [P, 2, 4, N])
        hT = sb("hT4", [P, 2, 4, N])
        ob = sb("ob", [N, EXPERTS, C])
        ps1 = [ctx.enter_context(nc.psum_tensor(f"ps1_{s}", [P, 4, N], F32)) for s in range(2)]
        ps2 = [ctx.enter_context(nc.psum_tensor(f"ps2_{s}", [N, C], F32)) for s in range(2)]

        def sem(name):
            return ctx.enter_context(nc.semaphore(name))
        w1_landed = [sem(f"w1_landed{s}") for s in range(SLOTS)]
        w2_landed = [sem(f"w2_landed{s}") for s in range(SLOTS)]
        hidden_ready, hidden_biased, gelu_ready = sem("hidden_ready"), sem("hidden_biased"), sem("gelu_ready")
        out_ready, out_copied, out_stored = sem("out_ready"), sem("out_copied"), sem("out_stored")

        with nc.Block() as block:
            @block.sync
            def _(sp):
                sp.sem_inc(out_ready, SLOTS)
                sp.sem_inc(out_copied, 2)
                with sp.Fori(0, EXPERTS // SLOTS, 1) as i:
                    for s in range(SLOTS):
                        sp.wait_ge(out_ready, i * SLOTS + s + 1)
                        sp.dma_start(w1[:, s], io["e_w1"][ds((i * SLOTS + s) * P, P), :]).then_inc(w1_landed[s], 16)
                        sp.dma_start(w2[:, s], io["e_w2"][ds((i * SLOTS + s) * P, P), :]).then_inc(w2_landed[s], 16)
                sp.wait_ge(out_copied, EXPERTS + 2)
                sp.dma_start(outE_dram, ob[:]).then_inc(out_stored, 16)
                sp.wait_ge(out_stored, 16)

            @block.tensor
            def _(pe):
                with pe.Fori(0, EXPERTS // SLOTS, 1) as i:
                    for s in range(SLOTS):
                        pe.wait_ge(w1_landed[s], 16 * i + 16)
                        for c in range(4):
                            mm = nc.tensor.matmul(ps1[s % 2][:, c, :], w1[:, s, c * P:(c + 1) * P],
                                                  pooledT[:, :, ds(i * SLOTS + s, 1)].rearrange("p n e -> p (n e)"),
                                                  start=True, stop=True)
                        mm.then_inc(hidden_ready, 1)
                        pe.wait_ge(gelu_ready, i * SLOTS + s + 1)
                        pe.wait_ge(w2_landed[s], 16 * i + 16)
                        pe.wait_ge(out_copied, i * SLOTS + s + 1)
                        for c in range(4):
                            mm = nc.tensor.matmul(ps2[s % 2][:, 0:C], hT[:, s % 2, c, :], w2[:, s, c * C:(c + 1) * C],
                                                  start=(c == 0), stop=(c == 3))
                        mm.then_inc(out_ready, 1)

            @block.vector
            def _(dve):
                with dve.Fori(0, EXPERTS // SLOTS, 1) as i:
                    for s in range(SLOTS):
                        e = i * SLOTS + s
                        dve.wait_ge(hidden_ready, e + 1)
                        b = cst["e_b1"][:, ds(e * 4, 4)].unsqueeze(2).to_broadcast([P, 4, N])
                        nc.vector.tensor_tensor(h[:, s % 2], ps1[s % 2][:], b, ALU.add).then_inc(hidden_biased, 1)
                        dve.wait_ge(out_ready, e + SLOTS + 1)
                        nc.vector.tensor_tensor(ob[:, ds(e, 1), :].rearrange("p e c -> p (e c)"), ps2[s % 2][:, 0:C],
                                                cst["e_b2"][:, ds(e * C, C)], ALU.add).then_inc(out_copied, 1)

            @block.scalar
            def _(act):
                with act.Fori(0, EXPERTS // SLOTS, 1) as i:
                    for s in range(SLOTS):
                        e = i * SLOTS + s
                        act.wait_ge(hidden_biased, e + 1)
                        nc.scalar.activation(hT[:, s % 2], h[:, s % 2], ACT.Gelu).then_inc(gelu_ready, 1)


def scatter_attention_route(nc, io, t1_dram, sel_dram, outE_dram, out_dram):
    with ExitStack() as ctx:
        def sb(name, shape, dt=F32):
            return ctx.enter_context(nc.sbuf_tensor(name, shape, dt))

        cst = load_constants(nc, ctx, io, ["router_w", "router_b", "iota8", "r_w", "r_b", "ident", "eps", "ones"], "p5")
        V1 = C + 1
        xt = sb("xt5", [TT, IT, C])
        sel = sb("sel5", [EXPERTS, HW])
        oe = sb("oe5", [EXPERTS, C])
        val = sb("val5", [TT, IT, V1])
        uT = sb("uT5", [P, CHUNKS * CT])
        sq = sb("sq5", [P, 2, CT])
        peak = sb("peak5", [1, CHUNKS * CT], BF16)
        minus1 = sb("minus1", [1, TT], BF16)
        E = sb("E5", [TT, 4, CT])
        st = sb("st5", [TT, CH, 6])
        mv = sb("mv5", [TT, CH, 2])
        rs = sb("rs5", [TT, CH])
        rden = sb("rden5", [TT, CH])
        u4 = sb("u45", [TT, CH, C])
        u4T = sb("u4T5", [P, CT])
        lg = sb("lg5", [TT, CH, ROUTED])
        pr = sb("pr5", [TT, CH, ROUTED])
        red = sb("red5", [TT, CH])
        vals = sb("vals5", [TT, CH, 8])
        idx = sb("idx5", [TT, CH, 8], U32)
        idxf = sb("idxf5", [TT, CH, 8])
        share = sb("share5", [TT, CH, ROUTED])
        other = sb("other5", [TT, CH, ROUTED])
        shareT = sb("shareT5", [ROUTED, CT])
        bank = [ctx.enter_context(nc.psum_tensor(f"bank5_{k}", [P, 512], F32)) for k in range(8)]

        def sem(name, per=CHUNKS):
            return Turns(ctx.enter_context(nc.semaphore(name)), per)
        landed = sem("p5_landed", 48)
        stored = sem("p5_stored", 16)
        ones_set = sem("ones_set", 1)
        spread = sem("spread_ready5")
        var_ready = sem("var5_ready", 2 * CHUNKS)
        std_ready = sem("std5_ready", 2 * CHUNKS)
        u_ready = sem("u5_ready")
        u_turned = sem("u5_turned")
        uT_ready = sem("uT5_ready")
        sq_ready = sem("sq_ready")
        norm_ready = sem("norm_ready")
        peak_ready = sem("peak_ready")
        score_ready = sem("score_ready", CHUNKS * IT)
        exp_ready = sem("exp5_ready", CHUNKS * IT)
        mix_step = sem("mix_step", CHUNKS * IT)
        mix_read = sem("mix_read")
        u4_ready = sem("u4_ready")
        u4_turned = sem("u4_turned")
        u4T_ready = sem("u4T_ready")
        route_ready = sem("route_ready")
        lg_ready = sem("lg5_ready")
        pr_ready = sem("pr5_ready")
        share_ready = sem("share_ready")
        share_turned = sem("share_turned")
        shareT_ready = sem("shareT_ready")
        bias_ready = sem("bias_ready")
        expert_ready = sem("expert_ready", IT)
        expert_read = sem("expert_read", IT)
        out_ready = sem("out5_ready")
        chain = ctx.enter_context(nc.semaphore("dve5_step"))
        mix_chain = ctx.enter_context(nc.semaphore("mix_den_ready"))
        tick = ctx.enter_context(nc.semaphore("dve5_tick"))
        sp_tick = ctx.enter_context(nc.semaphore("sp5_tick"))
        pe_tick = ctx.enter_context(nc.semaphore("pe5_tick"))

        with nc.Block() as block:
            @block.sync
            def _(sp):
                with sp.Fori(0, N, 1) as n:
                    stored.wait(sp, n, 16)
                    sp.sem_inc(sp_tick, 1)
                    sp.dma_start(xt[:], image_view(t1_dram, n)).then_inc(landed.sem, 16)
                    sp.dma_start(sel[:], sel_dram[ds(n * EXPERTS, EXPERTS), :]).then_inc(landed.sem, 16)
                    sp.dma_start(oe[:], outE_dram[ds(n, 1)].rearrange("n e c -> (n e) c")).then_inc(landed.sem, 16)
                    out_ready.wait(sp, n, CHUNKS)
                    sp.sem_inc(sp_tick, 1)
                    sp.dma_start(image_view(out_dram, n), xt[:]).then_inc(stored.sem, 16)
                sp.wait_ge(stored.sem, 16 * N + 16)

            @block.gpsimd
            def _(pool):
                pool.sem_inc(stored.sem, 16)
                pool.memset(val[:, :, C:V1], 1.0).then_inc(ones_set.sem, 1)
                pool.memset(minus1[:], -1.0).then_inc(ones_set.sem, 1)

            @block.tensor
            def _(pe):
                pe.wait_ge(ones_set.sem, 2)
                with pe.Fori(0, N, 1) as n:
                    landed.wait(pe, n, 48)

                    def spread_out(j):
                        for a in range(CH):
                            t = j * CH + a
                            mm = nc.tensor.matmul(bank[j % 2][0:TT, a * C:(a + 1) * C], sel[:, t * TT:(t + 1) * TT],
                                                  oe[:], start=True, stop=True)
                        mm.then_inc(spread.sem, 1)

                    def norm_row(j):
                        sq_ready.wait(pe, n, j + 1)
                        nc.tensor.matmul(bank[4 + j % 2][0:1, 0:CT], cst["ones"][:, 0:1], sq[:, j % 2],
                                         start=True, stop=True).then_inc(norm_ready.sem, 1)
                    spread_out(0)
                    for j in range(CHUNKS):
                        if j + 1 < CHUNKS:
                            spread_out(j + 1)
                        u_ready.wait(pe, n, j + 1)
                        if j >= 2:
                            sq_ready.wait(pe, n, j - 1)
                        for a in range(CH):
                            tr = nc.tensor.transpose(bank[2 + j % 2][:, a * TT:(a + 1) * TT], val[:, j * CH + a, 0:C],
                                                     cst["ident"][0:TT, 0:TT])
                        tr.then_inc(u_turned.sem, 1)
                        norm_row(j)
                    peak_ready.wait(pe, n, CHUNKS)
                    pe.sem_inc(pe_tick, 1)
                    with pe.Fori(0, CHUNKS, 1) as j:
                        base = (n * CHUNKS + j) * IT

                        def score(t, j=j):
                            nc.tensor.matmul(bank[t % 4][0:TT, 0:CT], uT[:, t * TT:(t + 1) * TT],
                                             uT[:, ds(j * CT, CT)], start=True, stop=False)
                            nc.tensor.matmul(bank[t % 4][0:TT, 0:CT], minus1[:], peak[:, ds(j * CT, CT)],
                                             start=False, stop=True).then_inc(score_ready.sem, 1)
                        for t in range(3):
                            score(t)
                        for t in range(IT):
                            if t + 3 < IT:
                                score(t + 3)
                            pe.wait_ge(exp_ready.sem, base + t + 1)
                            if t == 0:
                                pe.wait_ge(mix_read.sem, n * CHUNKS + j + 1)
                            for a in range(CH):
                                mm = nc.tensor.matmul(bank[4 + a // 2][0:TT, (a % 2) * V1:(a % 2 + 1) * V1],
                                                      E[:, t % 4, a * TT:(a + 1) * TT], val[:, t, :],
                                                      start=(t == 0 and a % 2 == 0), stop=(t == IT - 1),
                                                      skip_group_check=True)
                            mm.then_inc(mix_step.sem, 1)
                    for j in range(CHUNKS):
                        u4_ready.wait(pe, n, j + 1)
                        for a in range(CH):
                            tr = nc.tensor.transpose(bank[0][:, a * TT:(a + 1) * TT], u4[:, a, :], cst["ident"][0:TT, 0:TT])
                        tr.then_inc(u4_turned.sem, 1)
                        u4T_ready.wait(pe, n, j + 1)
                        for a in range(CH):
                            mm = nc.tensor.matmul(bank[1][0:TT, a * ROUTED:(a + 1) * ROUTED],
                                                  u4T[:, a * TT:(a + 1) * TT], cst["router_w"][:], start=True, stop=True)
                        mm.then_inc(route_ready.sem, 1)

                        def experts(a):
                            for k in range(2):
                                mm = nc.tensor.matmul(bank[4 + 2 * (a % 2) + k][0:TT, 0:4 * C], u4T[:, a * TT:(a + 1) * TT],
                                                      cst["r_w"][:, k * 4 * C:(k + 1) * 4 * C], start=True, stop=True)
                            mm.then_inc(expert_ready.sem, 1)
                        experts(0)
                        experts(1)
                        share_ready.wait(pe, n, j + 1)
                        for a in range(CH):
                            tr = nc.tensor.transpose(bank[2][0:ROUTED, a * TT:(a + 1) * TT], share[:, a, :],
                                                     cst["ident"][0:TT, 0:TT])
                        tr.then_inc(share_turned.sem, 1)
                        shareT_ready.wait(pe, n, j + 1)
                        for a in range(CH):
                            mm = nc.tensor.matmul(bank[3][0:TT, a * C:(a + 1) * C], shareT[:, a * TT:(a + 1) * TT],
                                                  cst["r_b"][:], start=True, stop=True)
                        mm.then_inc(bias_ready.sem, 1)
                        for a in range(2, CH):
                            expert_read.wait(pe, n, j * CH + a - 1)
                            experts(a)
                        if j + 1 < CHUNKS:
                            out_ready.wait(pe, n, j + 1)

            @block.scalar
            def _(act):
                S = nc.scalar
                with act.Fori(0, N, 1) as n:
                    def root(k):
                        var_ready.wait(act, n, k)
                        S.activation(rs[:], mv[:, :, 1], ACT.Sqrt, bias=cst["eps"][0:TT, 0:1]).then_inc(std_ready.sem, 1)
                    for j in range(CHUNKS):
                        root(j + 1)
                        u_turned.wait(act, n, j + 1)
                        S.copy(uT[:, j * CT:(j + 1) * CT], bank[2 + j % 2][:, 0:CT]).then_inc(uT_ready.sem, 1)
                        S.activation(sq[:, j % 2], bank[2 + j % 2][:, 0:CT], ACT.Square).then_inc(sq_ready.sem, 1)
                        norm_ready.wait(act, n, j + 1)
                        S.copy(peak[:, j * CT:(j + 1) * CT], bank[4 + j % 2][0:1, 0:CT]).then_inc(peak_ready.sem, 1)
                    with act.Fori(0, CHUNKS, 1) as j:
                        base = (n * CHUNKS + j) * IT
                        for t in range(IT):
                            act.wait_ge(score_ready.sem, base + t + 1)
                            act.wait_ge(mix_step.sem, base + t + 1)
                            S.activation(E[:, t % 4], bank[t % 4][0:TT, 0:CT], ACT.Exp)\
                                .then_inc(exp_ready.sem, 1)
                    for j in range(CHUNKS):
                        root(CHUNKS + j + 1)
                        u4_turned.wait(act, n, j + 1)
                        S.copy(u4T[:], bank[0][:, 0:CT]).then_inc(u4T_ready.sem, 1)
                        lg_ready.wait(act, n, j + 1)
                        S.activation(pr[:], lg[:], ACT.Exp).then_inc(pr_ready.sem, 1)
                        share_turned.wait(act, n, j + 1)
                        S.copy(shareT[:], bank[2][0:ROUTED, 0:CT]).then_inc(shareT_ready.sem, 1)

            @block.vector
            def _(dve):
                V = nc.vector
                dve.sem_inc(mix_read.sem, 1)
                dve.sem_inc(mix_step.sem, 4)
                cc = Chain(dve, chain, 0)
                with dve.Fori(0, N, 1) as n:
                    cc.turn, cc.per, cc.k = n, P5_LINKS, 0

                    def norm(j, out, k, ready):
                        for a in range(CH):
                            ins = V.bn_stats(st[:, a], xt[:, j * CH + a, :])
                        cc.link(ins)
                        dve.sem_inc(tick, 1)
                        for a in range(CH):
                            ins = V.bn_aggr(mv[:, a], st[:, a])
                        ins.then_inc(var_ready.sem, 1)
                        std_ready.wait(dve, n, k)
                        cc.link(V.reciprocal(rs[:], rs[:]))
                        for a in range(CH):
                            ins = V.tensor_scalar(out(a), xt[:, j * CH + a, :], mv[:, a, 0:1], rs[:, a:a + 1],
                                                  ALU.subtract, ALU.mult)
                        ins.then_inc(ready.sem, 1)

                    for j in range(CHUNKS):
                        x = xt[:, j * CH:(j + 1) * CH, :]
                        spread.wait(dve, n, j + 1)
                        cc.link(V.tensor_tensor(x, x, bank[j % 2][0:TT, 0:CH * C].rearrange("p (a c) -> p a c", a=CH),
                                                ALU.add))
                        norm(j, lambda a: val[:, j * CH + a, 0:C], j + 1, u_ready)
                    with dve.Fori(0, CHUNKS, 1) as j:
                        dve.wait_ge(mix_step.sem, (n * CHUNKS + j + 1) * IT + 4)
                        q = n * CHUNKS + j
                        for k in range(2):
                            ins = V.reciprocal(rden[:, 2 * k:2 * k + 2], bank[4 + k][0:TT, 0:2 * V1]
                                               .rearrange("p (a c) -> p a c", a=2)[:, :, C])
                        ins.then_inc(mix_chain, 1)
                        dve.wait_ge(mix_chain, q + 1)
                        for a in range(CH):
                            x = xt[:, ds(j * CH + a, 1), :].rearrange("p a c -> p (a c)")
                            ins = V.scalar_tensor_tensor(x, bank[4 + a // 2][0:TT, (a % 2) * V1:(a % 2) * V1 + C],
                                                         rden[:, a:a + 1], x, ALU.mult, ALU.add)
                        ins.then_inc(mix_read.sem, 1)
                    dve.wait_ge(mix_read.sem, n * CHUNKS + CHUNKS + 1)
                    for j in range(CHUNKS):
                        norm(j, lambda a: u4[:, a, :], CHUNKS + j + 1, u4_ready)
                        route_ready.wait(dve, n, j + 1)
                        rb = cst["router_b"][0:TT, :].unsqueeze(1).to_broadcast([TT, CH, ROUTED])

                        def wide(v):
                            return v.unsqueeze(2).to_broadcast([TT, CH, ROUTED])
                        cc.link(V.tensor_tensor(lg[:], bank[1][0:TT, 0:CH * ROUTED].rearrange("p (a e) -> p a e", a=CH),
                                                rb, ALU.add))
                        cc.link(V.tensor_reduce(red[:], lg[:], AX.X, ALU.max))
                        V.tensor_tensor(lg[:], lg[:], wide(red[:]), ALU.subtract).then_inc(lg_ready.sem, 1)
                        pr_ready.wait(dve, n, j + 1)
                        cc.link(V.tensor_reduce(red[:], pr[:], AX.X, ALU.add))
                        cc.link(V.reciprocal(red[:], red[:]))
                        cc.link(V.tensor_tensor(pr[:], pr[:], wide(red[:]), ALU.mult))
                        dve.sem_inc(tick, 1)
                        for a in range(CH):
                            ins = V.max(vals[:, a], pr[:, a])
                        cc.link(ins)
                        dve.sem_inc(tick, 1)
                        for a in range(CH):
                            ins = V.max_index(idx[:, a], vals[:, a], pr[:, a])
                        cc.link(ins)
                        cc.link(V.tensor_copy(idxf[:], idx[:]))
                        cc.link(V.tensor_tensor(red[:], vals[:, :, 0], vals[:, :, 1], ALU.add))
                        cc.link(V.reciprocal(red[:], red[:]))
                        io8 = cst["iota8"][0:TT, :].unsqueeze(1).to_broadcast([TT, CH, ROUTED])
                        cc.link(V.tensor_tensor(share[:], io8, wide(idxf[:, :, 0]), ALU.is_equal))
                        cc.link(V.tensor_tensor(share[:], share[:], wide(vals[:, :, 0]), ALU.mult))
                        cc.link(V.tensor_tensor(other[:], io8, wide(idxf[:, :, 1]), ALU.is_equal))
                        cc.link(V.tensor_tensor(other[:], other[:], wide(vals[:, :, 1]), ALU.mult))
                        cc.link(V.tensor_tensor(share[:], share[:], other[:], ALU.add))
                        V.tensor_tensor(share[:], share[:], wide(red[:]), ALU.mult).then_inc(share_ready.sem, 1)
                        share_ready.wait(dve, n, j + 1)
                        x = xt[:, j * CH:(j + 1) * CH, :]
                        bias_ready.wait(dve, n, j + 1)
                        cc.link(V.tensor_tensor(x, x, bank[3][0:TT, 0:CH * C].rearrange("p (a c) -> p a c", a=CH), ALU.add))
                        for a in range(CH):
                            xa = xt[:, j * CH + a, :]
                            expert_ready.wait(dve, n, j * CH + a + 1)
                            for e in range(ROUTED):
                                ins = V.scalar_tensor_tensor(
                                    xa, bank[4 + 2 * (a % 2) + e // 4][0:TT, (e % 4) * C:(e % 4 + 1) * C],
                                    share[:, a, e:e + 1], xa, ALU.mult, ALU.add)
                                if e < ROUTED - 1:
                                    cc.link(ins)
                                else:
                                    ins.then_inc(expert_read.sem, 1)
                        expert_read.wait(dve, n, (j + 1) * CH)
                        dve.sem_inc(out_ready.sem, 1)
                    assert cc.k == P5_LINKS, cc.k


def build(nc, io, out):
    def dram(name, shape):
        return nc.dram_tensor(name, shape, F32, kind="Internal").ap()
    flat_out = out.rearrange("a b c d -> (a b c) d")
    patch_table = dram("patch_table", [N * POS, GROUPS * 4 * CG])
    feat_dram = dram("features", [C, T])
    x2_dram, t1_dram = dram("x2_dram", [T, C]), dram("t1_dram", [T, C])
    sel_dram, outE_dram = dram("sel_dram", [N * EXPERTS, HW]), dram("outE_dram", [N, EXPERTS, C])
    patches_and_features(nc, io, patch_table, feat_dram)
    deformable_and_mlp(nc, io, patch_table, feat_dram, x2_dram)
    with nc.sbuf_tensor("pooledT", [P, N, EXPERTS], F32) as pooledT:
        norm_conv_attention_gate(nc, io, pooledT, x2_dram, t1_dram, sel_dram)
        pooled_experts(nc, io, pooledT, outE_dram)
    scatter_attention_route(nc, io, t1_dram, sel_dram, outE_dram, flat_out)


def lay_out(np, a):
    f = np.float32
    x = a["x"]

    def rows(v, k=P):
        return np.broadcast_to(v.reshape(1, -1), (k, v.size))

    def cols(v):
        return v.reshape(-1, P).T
    io = {}
    xT = np.zeros((N, C, XPAD), f)
    xT[:, :, :WP * WP] = np.pad(x, ((0, 0), (1, 1), (1, 1), (0, 0))).transpose(0, 3, 1, 2).reshape(N, C, WP * WP)
    io["xT"] = xT
    io["x"] = x.reshape(T, C)
    io["ident"] = np.eye(P, dtype=f)
    io["eps"] = np.full((P, 1), 1e-5, f)
    L = {k[8:]: v for k, v in a.items() if k.startswith("L0_conv_")}
    io["w_in"] = L["w_in"]
    bias4 = np.zeros((4, 4 * C), f)
    for k in range(4):
        bias4[k, k * C:(k + 1) * C] = L["b_in"]
    io["bias_in4"] = bias4
    inside = np.zeros(XPAD, f)
    inside[:WP * WP] = np.pad(np.ones((H, W), f), 1).reshape(-1)
    io["interior4"] = np.stack([inside[c:c + POS] for c in CORNER])
    io["dw_w"] = L["dw_w"].reshape(C, 9)
    for k in ("dw_b", "bn_g", "bn_b", "bn_m", "bn_v"):
        io[k] = L[k].reshape(C, 1)
    io["w_om"] = np.concatenate([L["w_off"], L["w_msk"]], 1)
    io["b_om"] = rows(np.concatenate([L["b_off"], L["b_msk"]]))
    grid = np.zeros((GROUPS, POINTS, 2), f)
    grid[:, :, 0] = np.arange(POINTS) // 3 - 1
    grid[:, :, 1] = np.arange(POINTS) % 3 - 1
    io["grid"] = rows(np.concatenate([grid.reshape(-1), np.zeros(GP, f)]))
    tok = np.arange(T).reshape(TILES, P).T
    io["tok_base"] = (np.stack([tok % W, tok // W % H], -1) + 0.5).astype(f).reshape(P, TILES * 2)
    io["row_base"] = (tok // HW * (POS * GROUPS)).astype(f)
    io["group_col"] = rows(np.repeat(np.arange(GROUPS), POINTS).astype(f))
    io["w_out"] = L["w_out"]
    for k in ("b_out", "ln1_g", "ln1_b", "gamma1", "b_fc2", "ln2_g", "ln2_b", "gamma2"):
        io[k] = rows(L[k])
    io["w_fc1"] = L["w_fc1"]
    io["b_fc1"] = cols(L["b_fc1"])
    io["w_fc2"] = L["w_fc2"].reshape(4, P, C).transpose(1, 0, 2).reshape(P, 4 * C)
    io["kernelT"] = a["L1_conv_kernel"].reshape(9, C, C).transpose(2, 0, 1).reshape(C, 9 * C)
    io["conv_bias"] = a["L1_conv_bias"].reshape(C, 1)
    io["W"] = a["L1_conv_W"]
    io["group_avg"] = np.kron(np.eye(32), np.full((4, 4), 0.25)).astype(f)
    for k in "qkv":
        io["W" + k] = a["L2_attn_W" + k]
        io["b" + k] = a["L2_attn_b" + k].reshape(C, 1)
    io["gate_wT"] = a["L2_ffn_gate_w"].T
    io["gate_b"] = a["L2_ffn_gate_b"].reshape(EXPERTS, 1)
    w1, w2 = a["L2_ffn_weight1"], a["L2_ffn_weight2"]
    io["e_w1"] = w1[:, :C].reshape(EXPERTS * C, HID)
    io["e_b1"] = w1[:, C].reshape(EXPERTS, 4, P).transpose(2, 0, 1).reshape(P, EXPERTS * 4)
    io["e_w2"] = w2[:, :HID].reshape(EXPERTS, 4, P, C).transpose(0, 2, 1, 3).reshape(EXPERTS * P, 4 * C)
    io["e_b2"] = rows(w2[:, HID], N)
    io["router_w"] = a["L3_ffn_router_w"]
    io["router_b"] = rows(a["L3_ffn_router_b"])
    io["iota8"] = rows(np.arange(ROUTED, dtype=f))
    io["r_w"] = a["L3_ffn_expert_w"].transpose(1, 0, 2).reshape(C, ROUTED * C)
    io["r_b"] = a["L3_ffn_expert_b"]
    io["ones"] = np.ones((P, 1), f)
    return {k: np.ascontiguousarray(v) for k, v in io.items()}


def kernel(**inputs):
    import numpy as _np
    import concourse.bacc as _bacc
    from concourse import mybir as _mybir
    from concourse.bass_utils import run_bass_kernel_spmd as _run

    nc = _bacc.Bacc("TRN2", target_bir_lowering=False, num_devices=1)
    laid = lay_out(_np, {k: _np.asarray(v) for k, v in inputs.items()})
    arrays, io = {}, {}
    for name, a in laid.items():
        arrays[f"in_{name}"] = a
        io[name] = nc.dram_tensor(f"in_{name}", a.shape, _mybir.dt.from_np(a.dtype), kind="ExternalInput").ap()
    out = nc.dram_tensor("out_0_dram", (N, H, W, C), _mybir.dt.float32, kind="ExternalOutput").ap()
    build(nc, io, out)
    r = _run(nc, [arrays], core_ids=[0])
    return r.results[0]["out_0_dram"]
```

```python
from contextlib import ExitStack

import concourse.bass as bass
from concourse import mybir

F32 = mybir.dt.float32
U32 = mybir.dt.uint32
BF16 = mybir.dt.bfloat16
F16 = mybir.dt.float16
ALU = mybir.AluOpType
ACT = mybir.ActivationFunctionType
AX = mybir.AxisListType
ds = bass.ds

N, H, W, C = 8, 56, 56, 128
HW = H * W
T = N * HW
P = 128
WP = W + 2
GROUPS, POINTS = 4, 9
GP = GROUPS * POINTS
CG = C // GROUPS
CORNER = (0, 1, WP, WP + 1)
POS_TILES = -(-((H + 1) * WP) // (4 * P)) * 4
POS = POS_TILES * P
XPAD = POS + WP + 2
STAGE = P + WP + 1
TILES = T // P
HID = 4 * C
MAGIC = 12582912.0


class Chain:

    def __init__(self, eng, sem, per):
        self.eng, self.sem, self.per, self.k, self.turn = eng, sem, per, 0, 0

    def begin(self, turn):
        assert self.k in (0, self.per), (self.k, self.per)
        self.turn, self.k = turn, 0

    def link(self, ins):
        ins.then_inc(self.sem, 1)
        self.k += 1
        self.eng.wait_ge(self.sem, self.turn * self.per + self.k)


def load_constants(nc, ctx, io, names, tag):
    tiles = {}
    for name in names:
        src = io[name]
        tiles[name] = ctx.enter_context(nc.sbuf_tensor(f"{tag}_{name}", list(src.shape), F32))
    s_const = ctx.enter_context(nc.semaphore(f"{tag}_consts_landed"))
    with nc.Block() as block:
        @block.sync
        def _(sp):
            for name in names:
                sp.dma_start(tiles[name][:], io[name]).then_inc(s_const, 16)
            sp.wait_ge(s_const, 16 * len(names))
    return tiles


def patches_and_features(nc, io, patch_table, feat_dram):
    with ExitStack() as ctx:
        def sb(name, shape, dt=F32):
            return ctx.enter_context(nc.sbuf_tensor(name, shape, dt))

        def sem(name):
            return ctx.enter_context(nc.semaphore(name))

        cst = load_constants(nc, ctx, io, ["w_in", "bias_in12", "interior12", "part12", "dw_w", "dw_b", "bn_g", "bn_b",
                                           "bn_m", "bn_v", "eps"], "p1")
        image = sb("image", [P, XPAD])
        conv = sb("conv", [P, H, W])
        feat = sb("feat", [P, HW])
        stage = sb("stage", [P, 4, STAGE])
        inside = sb("inside", [12, 4, P], BF16)
        bias_parts = sb("bias_parts", [12, 4 * C], BF16)
        part = sb("part", [12, 4 * C], BF16)
        rest = sb("rest", [12, 4 * C])
        picked = sb("picked", [12, 4 * C])
        patch = sb("patch", [P, 4, GROUPS, 4, CG])
        bn_scale = sb("bn_scale", [P, 1])
        bn_bias = sb("bn_bias", [P, 1])
        bn_std = sb("bn_std", [P, 1])
        ps = [ctx.enter_context(nc.psum_tensor(f"ps_patch{s}", [P, 4, C], F32)) for s in range(4)]

        image_landed = sem("image_landed")
        conv_done = sem("conv_done")
        conv_read = sem("conv_read")
        feat_stored = sem("feat_stored")
        staged = sem("staged")
        projected = sem("projected")
        patch_copied = sem("patch_copied")
        patch_stored = [sem(f"patch_stored{s}") for s in range(4)]
        dve_step = sem("p1_dve_step")
        bn_ready = sem("bn_ready")
        bn_root = sem("bn_root")
        QUADS = POS_TILES // 4
        with nc.Block() as block:
            @block.sync
            def _(sp):
                with sp.Fori(0, N, 1) as n:
                    sp.wait_ge(conv_done, n + 1)
                    sp.dma_start(image[:], io["xT"][ds(n, 1)].rearrange("a p c -> (a p) c"))\
                        .then_inc(image_landed, 16)
                    with sp.Fori(0, QUADS, 1) as i:
                        for s in range(4):
                            sp.wait_ge(patch_copied, n * POS_TILES + i * 4 + s + 1)
                            sp.dma_start(patch_table[ds(n * POS + (i * 4 + s) * P, P), :],
                                         patch[:, s].rearrange("p g k c -> p (g k c)"))\
                                .then_inc(patch_stored[s], 16)
                for s in range(4):
                    sp.wait_ge(patch_stored[s], 16 * N * QUADS + 16)

            @block.scalar
            def _(act):
                nc.scalar.activation(bn_std[:], cst["bn_v"][:], ACT.Sqrt, bias=cst["eps"][:, 0:1])\
                    .then_inc(bn_root, 1)
                with act.Fori(0, N, 1) as n:
                    act.wait_ge(image_landed, 16 * (n + 1))

                    def fill(i, s):
                        t = i * 4 + s
                        nc.scalar.copy(stage[:, s], image[:, ds(t * P, STAGE)]).then_inc(staged, 1)
                        nc.scalar.copy(inside[:, s], cst["interior12"][:, ds(t * P, P)]).then_inc(staged, 1)

                    def copy_out(i, s):
                        act.wait_ge(projected, n * POS_TILES + i * 4 + s + 1)
                        act.wait_ge(patch_stored[s], (n * QUADS + i) * 16 + 16)
                        nc.scalar.copy(patch[:, s].rearrange("p g k c -> p k g c"),
                                       ps[s][:].rearrange("p k (g c) -> p k g c", g=GROUPS)).then_inc(patch_copied, 1)

                    def pair(step, i, s):
                        step(i, s)
                        step(i, s + 1)
                    pair(fill, 0, 0)
                    with act.Fori(0, QUADS - 1, 1) as i:
                        pair(fill, i, 2)
                        pair(copy_out, i, 0)
                        pair(fill, i + 1, 0)
                        pair(copy_out, i, 2)
                    pair(fill, QUADS - 1, 2)
                    pair(copy_out, QUADS - 1, 0)
                    pair(copy_out, QUADS - 1, 2)
                    act.wait_ge(conv_done, n + 2)
                    act.wait_ge(bn_ready, 1)
                    act.wait_ge(feat_stored, 16 * n + 16)
                    nc.scalar.activation(feat[:], conv[:].rearrange("p h w -> p (h w)"), ACT.Gelu,
                                         bias=bn_bias[:, 0:1], scale=bn_scale[:, 0:1]).then_inc(conv_read, 1)
                    act.wait_ge(conv_read, n + 2)
                    act.dma_start(feat_dram[:, ds(n * HW, HW)], feat[:]).then_inc(feat_stored, 16)
                act.wait_ge(feat_stored, 16 * N + 16)

            @block.gpsimd
            def _(pool):
                pool.sem_inc(feat_stored, 16)
                pool.sem_inc(conv_read, 1)
                pool.sem_inc(conv_done, 1)
                for s in range(4):
                    pool.sem_inc(patch_stored[s], 16)

            @block.tensor
            def _(pe):
                pe.wait_ge(bn_ready, 1)
                with pe.Fori(0, N, 1) as n:
                    with pe.Fori(0, QUADS, 1) as i:
                        for s in range(4):
                            pe.wait_ge(staged, 2 * (n * POS_TILES + i * 4 + s) + 2)
                            for k, step in enumerate(CORNER):
                                nc.tensor.matmul(ps[s][:, k, :], stage[:, s, step:step + P], cst["w_in"][:],
                                                 start=(k == 0), stop=False, skip_group_check=True)
                            nc.tensor.matmul(ps[s][:].rearrange("p k c -> p (k c)"), inside[:, s],
                                             bias_parts[:], start=False, stop=True, skip_group_check=True)\
                                .then_inc(projected, 1)

            @block.vector
            def _(dve):
                step = Chain(dve, dve_step, 4 + 9)
                step.begin(0)
                left = cst["bias_in12"]
                for k in range(3):
                    step.link(nc.vector.tensor_copy(part[:], left[:]))
                    keep = cst["part12"][:, k:k + 1]
                    if k == 0:
                        step.link(nc.vector.tensor_scalar(picked[:], part[:], keep, None, ALU.mult))
                    else:
                        out = bias_parts if k == 2 else picked
                        step.link(nc.vector.scalar_tensor_tensor(out[:], part[:], keep, picked[:], ALU.mult, ALU.add))
                    step.link(nc.vector.tensor_tensor(rest[:], left[:], part[:], ALU.subtract))
                    left = rest
                dve.wait_ge(bn_root, 1)
                step.link(nc.vector.reciprocal(bn_scale[:], bn_std[:]))
                step.link(nc.vector.tensor_tensor(bn_scale[:], bn_scale[:], cst["bn_g"][:], ALU.mult))
                step.link(nc.vector.tensor_tensor(bn_bias[:], cst["dw_b"][:], cst["bn_m"][:], ALU.subtract))
                step.link(nc.vector.tensor_tensor(bn_bias[:], bn_bias[:], bn_scale[:], ALU.mult))
                nc.vector.tensor_tensor(bn_bias[:], bn_bias[:], cst["bn_b"][:], ALU.add).then_inc(bn_ready, 1)
                rows = image[:, 0:WP * WP].rearrange("p (h w) -> p h w", w=WP)
                with dve.Fori(0, N, 1) as n:
                    dve.wait_ge(image_landed, 16 * (n + 1))
                    dve.wait_ge(conv_read, n + 1)
                    for k in range(9):
                        view = rows[:, k // 3:k // 3 + H, k % 3:k % 3 + W]
                        tap = cst["dw_w"][:, k:k + 1]
                        if k == 0:
                            ins = nc.vector.tensor_scalar(conv[:], view, tap, None, ALU.mult)
                        else:
                            ins = nc.vector.scalar_tensor_tensor(conv[:], view, tap, conv[:], ALU.mult, ALU.add)
                        if k < 8:
                            ins.then_inc(dve_step, 1)
                            dve.wait_ge(dve_step, 13 + n * 8 + k + 1)
                    ins.then_inc(conv_done, 1)


FRONT, BACK = 15, 13


def deformable_and_mlp(nc, io, patch_table, feat_dram, x2_dram):
    with ExitStack() as ctx:
        def sb(name, shape, dt=F32):
            return ctx.enter_context(nc.sbuf_tensor(name, shape, dt))

        def sem(name):
            return ctx.enter_context(nc.semaphore(name))

        cst = load_constants(nc, ctx, io, ["w_om", "b_om", "grid", "tok_base", "row_base", "group_col", "w_out",
                                           "b_out", "ln1_g", "ln1_b", "gamma1", "w_fc1", "b_fc1", "w_fc2",
                                           "b_fc2", "ln2_g", "ln2_b", "gamma2", "ident", "eps"], "p2")
        featT = sb("featT", [P, 2, P])
        xin = sb("xin", [P, 2, C])
        om = sb("om", [P, 3 * GP])
        u = sb("u", [P, GP, 2])
        fl = sb("fl", [P, GP, 2])
        fr = sb("fr", [P, GP, 2])
        lin = sb("lin", [P, GP])
        idx = sb("idx", [P, 2, GP], U32)
        mx = sb("mx", [P, GROUPS])
        lg = sb("lg", [P, GROUPS, POINTS])
        ex = sb("ex", [P, GROUPS, POINTS])
        ssum = sb("ssum", [P, GROUPS])
        msk = sb("msk", [P, GP])
        lo = sb("lo", [P, GP])
        hi = sb("hi", [P, GP])
        wts = sb("wts", [P, 2, GP, 4])
        got = sb("got", [P, 2, GP, 4 * CG])
        samp = sb("samp", [P, C])
        sampT = sb("sampT", [P, P])
        y = sb("y", [P, C])
        st = sb("st", [P, 6])
        mv = sb("mv", [P, 2])
        rs = sb("rs", [P, 1])
        x1 = sb("x1", [P, C])
        x1T = sb("x1T", [P, P])
        hT = sb("hT", [P, 4, P])
        x2 = sb("x2", [P, 2, C])
        g1 = sb("g1", [P, C])
        b1 = sb("b1", [P, C])
        g2 = sb("g2", [P, C])
        b2 = sb("b2", [P, C])

        def pb(name, n):
            return ctx.enter_context(nc.psum_tensor(name, [P, n], F32))
        ps_om = [pb(f"ps_om{s}", 512) for s in range(2)]
        ps_t = pb("ps_t", 512)
        ps_y = pb("ps_y", 512)
        ps_h = pb("ps_h", 512)
        ps_m = pb("ps_m", 512)

        feat_landed = [sem(f"feat_landed{s}") for s in range(2)]
        x_landed = [sem(f"x_landed{s}") for s in range(2)]
        om_ready = sem("om_ready")
        om_read = sem("om_read")
        logits_ready = sem("logits_ready")
        exp_ready = sem("exp_ready")
        idx_ready = sem("idx_ready")
        weights_ready = sem("weights_ready")
        gathered = [sem(f"gathered{s}") for s in range(2)]
        gather_begun = sem("gather_begun")
        sampled = sem("sampled")
        samp_turned = sem("samp_turned")
        sampT_ready = sem("sampT_ready")
        y_ready = sem("y_ready")
        x1_ready = sem("x1_ready")
        x1_turned = sem("x1_turned")
        x1T_ready = sem("x1T_ready")
        h_ready = sem("h_ready")
        hT_ready = sem("hT_ready")
        m_ready = sem("m_ready")
        stats_turn = sem("stats_turn")
        var_ready = sem("var_ready")
        std_ready = sem("std_ready")
        x2_ready = sem("x2_ready")
        x2_stored = [sem(f"x2_stored{s}") for s in range(2)]
        front_step = sem("front_step")
        back_step = sem("back_step")
        setup_step = sem("setup_step")

        xf = io["x"]
        with nc.Block() as block:
            @block.sync
            def _(sp):
                def load(t, s):
                    sp.dma_start(featT[:, s], feat_dram[:, ds(t * P, P)]).then_inc(feat_landed[s], 16)
                    sp.dma_start(xin[:, s], xf[ds(t * P, P), :]).then_inc(x_landed[s], 16)

                def store(t, s):
                    sp.wait_ge(x2_ready, t + 1)
                    sp.dma_start(x2_dram[ds(t * P, P), :], x2[:, s]).then_inc(x2_stored[s], 16)
                for s in range(2):
                    load(s, s)
                with sp.Fori(0, TILES // 2 - 1, 1) as i:
                    for s in range(2):
                        store(2 * i + s, s)
                        load(2 * i + s + 2, s)
                for s in range(2):
                    store(TILES - 2 + s, s)
                for s in range(2):
                    sp.wait_ge(x2_stored[s], 16 * (TILES // 2) + 16)

            @block.gpsimd
            def _(pool):
                for s in range(2):
                    pool.sem_inc(x2_stored[s], 16)

                def gather(t, s, primed):
                    pool.wait_ge(idx_ready, t + 1)
                    if not primed:
                        pool.wait_ge(sampled, t - 1)
                        pool.sem_inc(gather_begun, 1)
                    for k in range(GP):
                        pool.indirect_dma_start(got[:, s, k], None, patch_table.rearrange("r (g c) -> (r g) c", g=GROUPS),
                                                bass.IndirectOffsetOnAxis(ap=idx[:, s, k:k + 1], axis=0))\
                            .then_inc(gathered[s], 16)
                for s in range(2):
                    gather(s, s, True)
                with pool.Fori(1, TILES // 2, 1) as i:
                    for s in range(2):
                        gather(2 * i + s, s, False)

            @block.tensor
            def _(pe):
                def front(t, s, primed=False):
                    pe.wait_ge(feat_landed[s], (t - s) * 8 + 16)
                    if not primed:
                        pe.wait_ge(om_read, t - 1)
                    nc.tensor.matmul(ps_om[s][:, 0:3 * GP], featT[:, s], cst["w_om"][:], start=True, stop=True)\
                        .then_inc(om_ready, 1)

                def back(t, s):
                    pe.wait_ge(sampled, t + 1)
                    nc.tensor.transpose(ps_t[:, 0:P], samp[:], cst["ident"][:]).then_inc(samp_turned, 1)
                    pe.wait_ge(sampT_ready, t + 1)
                    nc.tensor.matmul(ps_y[:, 0:C], sampT[:], cst["w_out"][:], start=True, stop=True)\
                        .then_inc(y_ready, 1)
                    pe.wait_ge(x1_ready, t + 1)
                    nc.tensor.transpose(ps_t[:, 0:P], x1[:], cst["ident"][:]).then_inc(x1_turned, 1)
                    pe.wait_ge(x1T_ready, t + 1)
                    for j in range(4):
                        mm = nc.tensor.matmul(ps_h[:, j * P:(j + 1) * P], cst["w_fc1"][:, j * P:(j + 1) * P], x1T[:],
                                              start=True, stop=True)
                    mm.then_inc(h_ready, 1)
                    pe.wait_ge(hT_ready, t + 1)
                    for j in range(4):
                        mm = nc.tensor.matmul(ps_m[:, 0:C], hT[:, j], cst["w_fc2"][:, j * C:(j + 1) * C],
                                              start=(j == 0), stop=(j == 3))
                    mm.then_inc(m_ready, 1)
                front(0, 0, True)
                front(1, 1, True)
                back(0, 0)
                with pe.Fori(0, TILES // 2 - 1, 1) as i:
                    front(2 * i + 2, 0)
                    back(2 * i + 1, 1)
                    front(2 * i + 3, 1)
                    back(2 * i + 2, 0)
                back(TILES - 1, 1)

            @block.scalar
            def _(act):
                def front(t):
                    act.wait_ge(logits_ready, t + 1)
                    nc.scalar.activation(ex[:], lg[:], ACT.Exp).then_inc(exp_ready, 1)

                def root(nth):
                    act.wait_ge(var_ready, nth)
                    nc.scalar.activation(rs[:], mv[:, 1:2], ACT.Sqrt, bias=cst["eps"][:, 0:1]).then_inc(std_ready, 1)

                def back(t):
                    act.wait_ge(samp_turned, t + 1)
                    nc.scalar.copy(sampT[:], ps_t[:, 0:P]).then_inc(sampT_ready, 1)
                    root(2 * t + 1)
                    act.wait_ge(x1_turned, t + 1)
                    nc.scalar.copy(x1T[:], ps_t[:, 0:P]).then_inc(x1T_ready, 1)
                    act.wait_ge(h_ready, t + 1)
                    for j in range(4):
                        g = nc.scalar.activation(hT[:, j], ps_h[:, j * P:(j + 1) * P], ACT.Gelu,
                                                 bias=cst["b_fc1"][:, j:j + 1])
                    g.then_inc(hT_ready, 1)
                    root(2 * t + 2)
                front(0)
                front(1)
                back(0)
                with act.Fori(0, TILES // 2 - 1, 1) as i:
                    front(2 * i + 2)
                    back(2 * i + 1)
                    front(2 * i + 3)
                    back(2 * i + 2)
                back(TILES - 1)

            @block.vector
            def _(dve):
                V = nc.vector
                fc = Chain(dve, front_step, FRONT)
                bc = Chain(dve, back_step, BACK)
                sc = Chain(dve, setup_step, 5)
                sc.begin(0)
                sc.link(V.tensor_tensor(g1[:], cst["ln1_g"][:], cst["gamma1"][:], ALU.mult))
                sc.link(V.tensor_tensor(b1[:], cst["ln1_b"][:], cst["gamma1"][:], ALU.mult))
                sc.link(V.tensor_tensor(g2[:], cst["ln2_g"][:], cst["gamma2"][:], ALU.mult))
                sc.link(V.tensor_tensor(b2[:], cst["ln2_b"][:], cst["gamma2"][:], ALU.mult))
                sc.link(V.tensor_tensor(cst["b_om"][:], cst["b_om"][:], cst["grid"][:], ALU.add))

                def front(t, s):
                    fc.begin(t)
                    dve.wait_ge(om_ready, t + 1)
                    V.tensor_tensor(om[:], ps_om[s][:, 0:3 * GP], cst["b_om"][:], ALU.add).then_inc(om_read, 1)
                    dve.wait_ge(om_read, t + 1)
                    logits = om[:, 2 * GP:3 * GP].rearrange("p (g k) -> p g k", g=GROUPS)
                    fc.link(V.tensor_reduce(mx[:], logits, AX.X, ALU.max))
                    V.tensor_tensor(lg[:], logits, mx[:].unsqueeze(2).to_broadcast([P, GROUPS, POINTS]),
                                    ALU.subtract).then_inc(logits_ready, 1)
                    base = cst["tok_base"][:, ds(t * 2, 2)].unsqueeze(1).to_broadcast([P, GP, 2])
                    fc.link(V.tensor_tensor(u[:], om[:, 0:2 * GP].rearrange("p (k c) -> p k c", c=2), base, ALU.add))
                    fc.link(V.tensor_scalar(u[:], u[:], -0.5, H + 0.5, ALU.max, ALU.min))
                    fc.link(V.tensor_scalar(fl[:], u[:], MAGIC, None, ALU.add))
                    fc.link(V.tensor_scalar(fl[:], fl[:], MAGIC, None, ALU.subtract))
                    fc.link(V.scalar_tensor_tensor(fr[:], u[:], 0.5, fl[:], ALU.add, ALU.subtract))
                    fc.link(V.scalar_tensor_tensor(lin[:], fl[:, :, 1], float(WP), fl[:, :, 0], ALU.mult, ALU.add))
                    fc.link(V.tensor_scalar(lin[:], lin[:], float(GROUPS), cst["row_base"][:, ds(t, 1)],
                                            ALU.mult, ALU.add))
                    V.tensor_tensor(idx[:, s], lin[:], cst["group_col"][:], ALU.add).then_inc(idx_ready, 1)
                    dve.wait_ge(exp_ready, t + 1)
                    fc.link(V.tensor_reduce(ssum[:], ex[:], AX.X, ALU.add))
                    fc.link(V.reciprocal(ssum[:], ssum[:]))
                    fc.link(V.tensor_tensor(msk[:].rearrange("p (g k) -> p g k", g=GROUPS), ex[:],
                                            ssum[:].unsqueeze(2).to_broadcast([P, GROUPS, POINTS]), ALU.mult))
                    fc.link(V.tensor_tensor(lo[:], msk[:], fr[:, :, 1], ALU.mult))
                    fc.link(V.tensor_tensor(hi[:], msk[:], lo[:], ALU.subtract))
                    fc.link(V.tensor_tensor(wts[:, s, :, 3], lo[:], fr[:, :, 0], ALU.mult))
                    fc.link(V.tensor_tensor(wts[:, s, :, 1], hi[:], fr[:, :, 0], ALU.mult))
                    V.tensor_tensor(wts[:, s, :, 2], lo[:], wts[:, s, :, 3], ALU.subtract).then_inc(weights_ready, 1)
                    V.tensor_tensor(wts[:, s, :, 0], hi[:], wts[:, s, :, 1], ALU.subtract).then_inc(weights_ready, 1)

                def norm(g, b, res, out, nth, ready):
                    bc.link(V.bn_stats(st[:], y[:]))
                    dve.sem_inc(stats_turn, 1)
                    V.bn_aggr(mv[:], st[:]).then_inc(var_ready, 1)
                    dve.wait_ge(std_ready, nth)
                    bc.link(V.reciprocal(rs[:], rs[:]))
                    bc.link(V.tensor_scalar(y[:], y[:], mv[:, 0:1], rs[:, 0:1], ALU.subtract, ALU.mult))
                    bc.link(V.tensor_tensor(y[:], y[:], g[:], ALU.mult))
                    bc.link(V.tensor_tensor(y[:], y[:], b[:], ALU.add))
                    V.tensor_tensor(out, y[:], res, ALU.add).then_inc(ready, 1)

                def back(t, s):
                    bc.begin(t)
                    dve.wait_ge(gathered[s], (t - s) * (8 * GP) + 16 * GP)
                    dve.wait_ge(weights_ready, 2 * t + 2)
                    v = got[:, s].rearrange("p k (q c) -> p (k q) c", q=4)
                    w = wts[:, s].rearrange("p k q -> p (k q)").unsqueeze(2).to_broadcast([P, GP * 4, CG])
                    bc.link(V.tensor_tensor(v, v, w, ALU.mult))
                    V.tensor_reduce(samp[:].rearrange("p (g c) -> p g c", g=GROUPS),
                                    got[:, s].rearrange("p (g k) (q c) -> p g c (k q)", g=GROUPS, q=4),
                                    AX.X, ALU.add).then_inc(sampled, 1)
                    dve.wait_ge(y_ready, t + 1)
                    dve.wait_ge(x_landed[s], (t - s) * 8 + 16)
                    bc.link(V.tensor_tensor(y[:], ps_y[:, 0:C], cst["b_out"][:], ALU.add))
                    norm(g1, b1, xin[:, s], x1[:], 2 * t + 1, x1_ready)
                    dve.wait_ge(m_ready, t + 1)
                    dve.wait_ge(x1_ready, t + 1)
                    dve.wait_ge(x2_stored[s], (t - s) * 8 + 16)
                    bc.link(V.tensor_tensor(y[:], ps_m[:, 0:C], cst["b_fc2"][:], ALU.add))
                    norm(g2, b2, x1[:], x2[:, s], 2 * t + 2, x2_ready)
                front(0, 0)
                front(1, 1)
                back(0, 0)
                with dve.Fori(0, TILES // 2 - 1, 1) as i:
                    front(2 * i + 2, 0)
                    back(2 * i + 1, 1)
                    front(2 * i + 3, 1)
                    back(2 * i + 2, 0)
                back(TILES - 1, 1)


TT = 2 * W
IT = HW // TT
CH = 4
CHUNKS = IT // CH
CT = CH * TT
CROWS = CT // W
EXPERTS, TOPK = 64, 8
ROUTED = 8
P3_LINKS, P5_LINKS = 51, 19


class Turns:

    def __init__(self, sem, per):
        self.sem, self.per = sem, per

    def wait(self, eng, n, k):
        eng.wait_ge(self.sem, n * self.per + k)


def image_view(dram, n):
    return dram[ds(n * HW, HW), :].rearrange("(a p) c -> p a c", p=TT)


def norm_conv_attention_gate(nc, io, pooledT, x2_dram, t1_dram, sel_dram):
    with ExitStack() as ctx:
        def sb(name, shape, dt=F32):
            return ctx.enter_context(nc.sbuf_tensor(name, shape, dt))

        cst = load_constants(nc, ctx, io, ["kernelT", "conv_bias", "W", "group_avg", "Wq", "bq", "Wk", "bk", "Wv",
                                           "bv", "gate_wT", "gate_b", "ident", "eps"], "p3")
        fused = sb("fused", [P, 9, C])
        fused_bias = sb("fused_bias", [P, 1])
        xt = sb("xt", [TT, IT, C])
        gimg = sb("gimg", [P, WP * WP])
        grows = gimg[:].rearrange("p (h w) -> p h w", w=WP)
        cstat = sb("cstat", [P, CHUNKS, 6])
        cmv = sb("cmv", [P, 2])
        gmean = sb("gmean", [P, 1])
        dev = sb("dev", [P, 1])
        spread = sb("spread", [P, 1])
        gstd = sb("gstd", [P, 1])
        cT = sb("cT", [P, 2, CT])
        st = sb("st3", [TT, CH, 6])
        mv = sb("mv3", [TT, CH, 2])
        rs = sb("rs3", [TT, CH])
        un = sb("un", [TT, 2, CH, C])
        uT = sb("uT", [P, CHUNKS, CT])
        ksb = sb("ksb", [P, CT])
        kv_junk = sb("kv_junk", [P, CT])
        kvp = sb("kvp", [P, CHUNKS])
        kv = sb("kv", [P, 1])
        bqkv = sb("bqkv", [P, 1])
        u2 = sb("u2", [TT, IT, C])
        u2T = sb("u2T", [P, 2, CT])
        lg = sb("lg3", [EXPERTS, HW])
        pr = sb("pr3", [EXPERTS, HW])
        rep = sb("rep3", [EXPERTS, HW])
        nmx = sb("nmx", [EXPERTS, 1])
        psum_e = sb("psum_e", [EXPERTS, 1])
        top = sb("top", [EXPERTS, 8])
        selT = sb("selT", [TT, 2, CH, EXPERTS])
        pooled = sb("pooled", [EXPERTS, C])
        bank = [ctx.enter_context(nc.psum_tensor(f"bank{k}", [P, 512], F32)) for k in range(8)]

        def sem(name, per=CHUNKS):
            return Turns(ctx.enter_context(nc.semaphore(name)), per)
        fuse_ready, fuse_copied, border_zeroed = sem("fuse_ready"), sem("fuse_copied"), sem("border_zeroed")
        image_done = sem("image_done", 1)
        x_landed = sem("x2_landed", 16)
        t1_stored = sem("t1_stored", 16)
        sel_stored = sem("sel_stored", 16)
        turned = sem("x2_turned")
        gimg_copied = sem("gimg_copied")
        stats_taken = sem("stats_taken")
        mean_ready = sem("mean_ready", 1)
        gmean_ready = sem("gmean_ready", 1)
        spread_ready = sem("spread_ready", 1)
        gvar_ready = sem("gvar_ready", 1)
        gstd_ready = sem("gstd_ready", 1)
        normed = sem("normed", 1)
        conv_ready = sem("conv_ready")
        cT_ready = sem("cT_ready")
        c_turned = sem("c_turned")
        var_ready = sem("var3_ready", 2 * CHUNKS)
        std_ready = sem("std3_ready", 2 * CHUNKS)
        u_ready = sem("u_ready")
        u_turned = sem("u_turned")
        uT_ready = sem("uT_ready")
        k_ready = sem("k_ready")
        v_ready = sem("v_ready")
        ksb_ready = sem("ksb_ready")
        kv_summed = sem("kv_summed")
        kv_ready = sem("kv_ready", 1)
        q_ready = sem("q_ready")
        qT_ready = sem("qT_ready")
        q_turned = sem("q_turned")
        u2_ready = sem("u2_ready")
        u2_turned = sem("u2_turned")
        u2T_ready = sem("u2T_ready")
        gate_ready = sem("gate_ready")
        lg_ready = sem("lg_ready")
        max_ready = sem("max_ready", 1)
        prob_ready = sem("prob_ready", 1)
        sel_ready = sem("sel_ready", 1)
        sel_turned = sem("sel_turned")
        selT_ready = sem("selT_ready")
        pool_step = sem("pool_step")
        pooled_copied = sem("pooled_copied", 1)
        pooled_turned = sem("pooled_turned", 1)
        chain = ctx.enter_context(nc.semaphore("dve3_step"))
        tick = ctx.enter_context(nc.semaphore("dve3_tick"))
        pe_tick = ctx.enter_context(nc.semaphore("pe3_tick"))
        sp_tick = ctx.enter_context(nc.semaphore("sp3_tick"))

        with nc.Block() as block:
            @block.sync
            def _(sp):
                with sp.Fori(0, N, 1) as n:
                    image_done.wait(sp, n, 1)
                    sp.sem_inc(sp_tick, 1)
                    sp.dma_start(xt[:], image_view(x2_dram, n)).then_inc(x_landed.sem, 16)
                    u2_ready.wait(sp, n, CHUNKS)
                    sp.sem_inc(sp_tick, 1)
                    sp.dma_start(image_view(t1_dram, n), xt[:]).then_inc(t1_stored.sem, 16)
                    sel_ready.wait(sp, n, 1)
                    sp.sem_inc(sp_tick, 1)
                    sp.dma_start(sel_dram[ds(n * EXPERTS, EXPERTS), :], pr[:]).then_inc(sel_stored.sem, 16)
                    t1_stored.wait(sp, n, 16)
                    sel_stored.wait(sp, n, 16)
                    sp.sem_inc(sp_tick, 1)

            @block.gpsimd
            def _(pool):
                pool.sem_inc(image_done.sem, 1)
                pool.memset(gimg[:], 0.0).then_inc(border_zeroed.sem, 1)

            @block.tensor
            def _(pe):
                for k in range(9):
                    nc.tensor.matmul(bank[k // 4][:, (k % 4) * C:(k % 4 + 1) * C], cst["kernelT"][:, k * C:(k + 1) * C],
                                     cst["W"][:], start=True, stop=True)
                nc.tensor.matmul(bank[3][:, 0:1], cst["W"][:], cst["conv_bias"][:], start=True, stop=True)\
                    .then_inc(fuse_ready.sem, 1)
                pe.wait_ge(fuse_copied.sem, 4)

                def turn(dst, src, parts):
                    for a in range(CH):
                        ins = nc.tensor.transpose(dst(a), src(a), cst["ident"][0:parts, 0:parts])
                    return ins

                def cols(b, a, rows=P):
                    return bank[b][0:rows, a * TT:(a + 1) * TT]

                with pe.Fori(0, N, 1) as n:
                    x_landed.wait(pe, n, 16)
                    for j in range(CHUNKS):
                        if j >= 2:
                            gimg_copied.wait(pe, n, j - 1)
                        turn(lambda a: cols(j % 2, a), lambda a: xt[:, j * CH + a, :], TT).then_inc(turned.sem, 1)
                    mean_ready.wait(pe, n, 1)
                    nc.tensor.matmul(bank[2][:, 0:1], cst["group_avg"][:], cmv[:, 0:1], start=True, stop=True)\
                        .then_inc(gmean_ready.sem, 1)
                    spread_ready.wait(pe, n, 1)
                    nc.tensor.matmul(bank[3][:, 0:1], cst["group_avg"][:], spread[:], start=True, stop=True)\
                        .then_inc(gvar_ready.sem, 1)
                    normed.wait(pe, n, 1)

                    def conv(j):
                        for k in range(9):
                            r = j * CROWS + k // 3
                            mm = nc.tensor.matmul(bank[j % 2][:, 0:CT], fused[:, k, :],
                                                  grows[:, r:r + CROWS, k % 3:k % 3 + W],
                                                  start=(k == 0), stop=(k == 8))
                        mm.then_inc(conv_ready.sem, 1)
                    conv(0)
                    for j in range(CHUNKS):
                        cT_ready.wait(pe, n, j + 1)
                        turn(lambda a: bank[2][0:TT, a * C:(a + 1) * C], lambda a: cT[:, j % 2, a * TT:(a + 1) * TT], P)\
                            .then_inc(c_turned.sem, 1)
                        if j + 1 < CHUNKS:
                            conv(j + 1)
                        u_ready.wait(pe, n, j + 1)
                        turn(lambda a: cols(3, a), lambda a: un[:, j % 2, a, :], TT).then_inc(u_turned.sem, 1)
                        uT_ready.wait(pe, n, j + 1)
                        if j:
                            kv_summed.wait(pe, n, j)
                        nc.tensor.matmul(bank[4][:, 0:CT], cst["Wk"][:], uT[:, j], start=True, stop=True)\
                            .then_inc(k_ready.sem, 1)
                        nc.tensor.matmul(bank[5][:, 0:CT], cst["Wv"][:], uT[:, j], start=True, stop=True)\
                            .then_inc(v_ready.sem, 1)

                    def query(j):
                        nc.tensor.matmul(bank[j % 2][:, 0:CT], cst["Wq"][:], uT[:, j], start=True, stop=True)\
                            .then_inc(q_ready.sem, 1)
                    query(0)
                    kv_summed.wait(pe, n, CHUNKS)
                    for j in range(CHUNKS):
                        qT_ready.wait(pe, n, j + 1)
                        turn(lambda a: bank[2][0:TT, a * C:(a + 1) * C], lambda a: cT[:, j % 2, a * TT:(a + 1) * TT], P)\
                            .then_inc(q_turned.sem, 1)
                        if j + 1 < CHUNKS:
                            query(j + 1)
                        u2_ready.wait(pe, n, j + 1)
                        turn(lambda a: cols(3, a), lambda a: u2[:, j * CH + a, :], TT).then_inc(u2_turned.sem, 1)
                        u2T_ready.wait(pe, n, j + 1)
                        if j:
                            lg_ready.wait(pe, n, j)
                        nc.tensor.matmul(bank[4][0:EXPERTS, 0:CT], cst["gate_wT"][:], u2T[:, j % 2],
                                         start=True, stop=True).then_inc(gate_ready.sem, 1)
                    sel_ready.wait(pe, n, 1)

                    pe.sem_inc(pe_tick, 1)

                    def turn_sel(j):
                        turn(lambda a: bank[j % 2][0:TT, a * EXPERTS:(a + 1) * EXPERTS],
                             lambda a: pr[:, (j * CH + a) * TT:(j * CH + a + 1) * TT], EXPERTS)\
                            .then_inc(sel_turned.sem, 1)
                    turn_sel(0)
                    for j in range(CHUNKS):
                        if j + 1 < CHUNKS:
                            turn_sel(j + 1)
                        selT_ready.wait(pe, n, j + 1)
                        for a in range(CH):
                            mm = nc.tensor.matmul(bank[5][0:EXPERTS, 0:C], selT[:, j % 2, a], u2[:, j * CH + a, :],
                                                  start=(j == 0 and a == 0), stop=(j == CHUNKS - 1 and a == CH - 1))
                        mm.then_inc(pool_step.sem, 1)
                    pooled_copied.wait(pe, n, 1)
                    pe.sem_inc(pe_tick, 1)
                    nc.tensor.transpose(bank[6][:, 0:EXPERTS], pooled[:], cst["ident"][0:EXPERTS, 0:EXPERTS])\
                        .then_inc(pooled_turned.sem, 1)

            @block.scalar
            def _(act):
                S = nc.scalar
                act.wait_ge(fuse_ready.sem, 1)
                for k in range(2):
                    S.copy(fused[:, 4 * k:4 * k + 4].rearrange("p k c -> p (k c)"), bank[k][:]).then_inc(fuse_copied.sem, 1)
                S.copy(fused[:, 8], bank[2][:, 0:C]).then_inc(fuse_copied.sem, 1)
                S.copy(fused_bias[:], bank[3][:, 0:1]).then_inc(fuse_copied.sem, 1)
                act.wait_ge(fuse_copied.sem, 4)
                act.wait_ge(border_zeroed.sem, 1)
                with act.Fori(0, N, 1) as n:
                    for j in range(CHUNKS):
                        turned.wait(act, n, j + 1)
                        S.copy(grows[:, 1 + j * CROWS:1 + (j + 1) * CROWS, 1:1 + W],
                               bank[j % 2][:, 0:CT].rearrange("p (h w) -> p h w", w=W)).then_inc(gimg_copied.sem, 1)
                    gvar_ready.wait(act, n, 1)
                    S.activation(gstd[:], bank[3][:, 0:1], ACT.Sqrt, bias=cst["eps"][:, 0:1]).then_inc(gstd_ready.sem, 1)

                    def root(k):
                        var_ready.wait(act, n, k)
                        S.activation(rs[:], mv[:, :, 1], ACT.Sqrt, bias=cst["eps"][0:TT, 0:1]).then_inc(std_ready.sem, 1)

                    def conv_out(j):
                        conv_ready.wait(act, n, j + 1)
                        S.activation(cT[:, j % 2], bank[j % 2][:, 0:CT], ACT.Identity, bias=fused_bias[:, 0:1])\
                            .then_inc(cT_ready.sem, 1)
                    conv_out(0)
                    for j in range(CHUNKS):
                        root(j + 1)
                        if j + 1 < CHUNKS:
                            conv_out(j + 1)
                        u_turned.wait(act, n, j + 1)
                        S.copy(uT[:, j], bank[3][:, 0:CT]).then_inc(uT_ready.sem, 1)
                        k_ready.wait(act, n, j + 1)
                        if j:
                            kv_summed.wait(act, n, j)
                        S.activation(ksb[:], bank[4][:, 0:CT], ACT.Identity, bias=cst["bk"][:, 0:1])\
                            .then_inc(ksb_ready.sem, 1)
                    kv_ready.wait(act, n, 1)

                    def query_out(j):
                        q_ready.wait(act, n, j + 1)
                        S.activation(cT[:, j % 2], bank[j % 2][:, 0:CT], ACT.Identity, bias=bqkv[:, 0:1],
                                     scale=kv[:, 0:1]).then_inc(qT_ready.sem, 1)
                    query_out(0)
                    for j in range(CHUNKS):
                        root(CHUNKS + j + 1)
                        if j + 1 < CHUNKS:
                            query_out(j + 1)
                        u2_turned.wait(act, n, j + 1)
                        S.copy(u2T[:, j % 2], bank[3][:, 0:CT]).then_inc(u2T_ready.sem, 1)
                        gate_ready.wait(act, n, j + 1)
                        S.activation(lg[:, j * CT:(j + 1) * CT], bank[4][0:EXPERTS, 0:CT], ACT.Identity,
                                     bias=cst["gate_b"][:, 0:1]).then_inc(lg_ready.sem, 1)
                    max_ready.wait(act, n, 1)
                    S.activation(lg[:], lg[:], ACT.Exp, bias=nmx[:, 0:1], accum_out=psum_e[:, 0:1])\
                        .then_inc(prob_ready.sem, 1)
                    for j in range(CHUNKS):
                        sel_turned.wait(act, n, j + 1)
                        if j >= 2:
                            pool_step.wait(act, n, j - 1)
                        S.copy(selT[:, j % 2].rearrange("p a e -> p (a e)"), bank[j % 2][0:TT, 0:CH * EXPERTS])\
                            .then_inc(selT_ready.sem, 1)
                    pool_step.wait(act, n, CHUNKS)
                    S.copy(pooled[:], bank[5][0:EXPERTS, 0:C]).then_inc(pooled_copied.sem, 1)
                    pooled_turned.wait(act, n, 1)
                    S.copy(pooledT[:, ds(n, 1), :].rearrange("p n e -> p (n e)"), bank[6][:, 0:EXPERTS])\
                        .then_inc(image_done.sem, 1)

            @block.vector
            def _(dve):
                V = nc.vector
                cc = Chain(dve, chain, 0)
                with dve.Fori(0, N, 1) as n:
                    cc.turn, cc.per, cc.k = n, P3_LINKS, 0
                    for j in range(CHUNKS):
                        gimg_copied.wait(dve, n, j + 1)
                        V.bn_stats(cstat[:, j], grows[:, 1 + j * CROWS:1 + (j + 1) * CROWS, 1:1 + W])\
                            .then_inc(stats_taken.sem, 1)
                    stats_taken.wait(dve, n, CHUNKS)
                    dve.sem_inc(tick, 1)
                    V.bn_aggr(cmv[:], cstat[:].rearrange("p j k -> p (j k)")).then_inc(mean_ready.sem, 1)
                    gmean_ready.wait(dve, n, 1)
                    cc.link(V.tensor_copy(gmean[:], bank[2][:, 0:1]))
                    cc.link(V.tensor_tensor(dev[:], cmv[:, 0:1], gmean[:], ALU.subtract))
                    V.scalar_tensor_tensor(spread[:], dev[:], dev[:, 0:1], cmv[:, 1:2], ALU.mult, ALU.add)\
                        .then_inc(spread_ready.sem, 1)
                    gstd_ready.wait(dve, n, 1)
                    gimg_copied.wait(dve, n, CHUNKS)
                    cc.link(V.reciprocal(gstd[:], gstd[:]))
                    inner = grows[:, 1:1 + H, 1:1 + W]
                    V.tensor_scalar(inner, inner, gmean[:, 0:1], gstd[:, 0:1], ALU.subtract, ALU.mult)\
                        .then_inc(normed.sem, 1)

                    def add_and_norm(j, out, k, ready):
                        x = xt[:, j * CH:(j + 1) * CH, :]
                        cc.link(V.tensor_tensor(x, x, bank[2][0:TT, 0:CH * C].rearrange("p (a c) -> p a c", a=CH), ALU.add))
                        for a in range(CH):
                            ins = V.bn_stats(st[:, a], xt[:, j * CH + a, :])
                        cc.link(ins)
                        dve.sem_inc(tick, 1)
                        for a in range(CH):
                            ins = V.bn_aggr(mv[:, a], st[:, a])
                        ins.then_inc(var_ready.sem, 1)
                        std_ready.wait(dve, n, k)
                        cc.link(V.reciprocal(rs[:], rs[:]))
                        for a in range(CH):
                            ins = V.tensor_scalar(out(a), xt[:, j * CH + a, :], mv[:, a, 0:1], rs[:, a:a + 1],
                                                  ALU.subtract, ALU.mult)
                        ins.then_inc(ready.sem, 1)

                    for j in range(CHUNKS):
                        c_turned.wait(dve, n, j + 1)
                        add_and_norm(j, lambda a: un[:, j % 2, a, :], j + 1, u_ready)
                        v_ready.wait(dve, n, j + 1)
                        ksb_ready.wait(dve, n, j + 1)
                        V.scalar_tensor_tensor(kv_junk[:], bank[5][:, 0:CT], cst["bv"][:, 0:1], ksb[:], ALU.add,
                                               ALU.mult, accum_out=kvp[:, j:j + 1]).then_inc(kv_summed.sem, 1)
                    kv_summed.wait(dve, n, CHUNKS)
                    cc.link(V.tensor_reduce(kv[:], kvp[:], AX.X, ALU.add))
                    V.tensor_tensor(bqkv[:], cst["bq"][:], kv[:], ALU.mult).then_inc(kv_ready.sem, 1)
                    for j in range(CHUNKS):
                        q_turned.wait(dve, n, j + 1)
                        add_and_norm(j, lambda a: u2[:, j * CH + a, :], CHUNKS + j + 1, u2_ready)
                    lg_ready.wait(dve, n, CHUNKS)
                    cc.link(V.tensor_reduce(nmx[:], lg[:], AX.X, ALU.max))
                    V.tensor_scalar(nmx[:], nmx[:], -1.0, None, ALU.mult).then_inc(max_ready.sem, 1)
                    prob_ready.wait(dve, n, 1)
                    dve.sem_inc(tick, 1)
                    cc.link(V.max(top[:], lg[:]))
                    dve.sem_inc(tick, 1)
                    cc.link(V.match_replace(rep[:], top[:], lg[:], 0.0))
                    cc.link(V.reciprocal(psum_e[:], psum_e[:]))
                    cc.link(V.tensor_tensor(rep[:], lg[:], rep[:], ALU.subtract))
                    V.tensor_scalar(pr[:], rep[:], psum_e[:, 0:1], None, ALU.mult).then_inc(sel_ready.sem, 1)
                    assert cc.k == P3_LINKS, cc.k


def pooled_experts(nc, io, pooledT, outE_dram):
    SLOTS = 4
    with ExitStack() as ctx:
        def sb(name, shape, dt=F32):
            return ctx.enter_context(nc.sbuf_tensor(name, shape, dt))

        cst = load_constants(nc, ctx, io, ["e_b1", "e_b2"], "p4")
        w1 = sb("w1", [P, SLOTS, HID])
        w2 = sb("w2", [P, SLOTS, 4 * C])
        h = sb("h4", [P, 2, 4, N])
        hT = sb("hT4", [P, 2, 4, N])
        ob = sb("ob", [N, EXPERTS, C])
        ps1 = [ctx.enter_context(nc.psum_tensor(f"ps1_{s}", [P, 4, N], F32)) for s in range(2)]
        ps2 = [ctx.enter_context(nc.psum_tensor(f"ps2_{s}", [N, C], F32)) for s in range(2)]

        def sem(name):
            return ctx.enter_context(nc.semaphore(name))
        w1_landed = [sem(f"w1_landed{s}") for s in range(SLOTS)]
        w2_landed = [sem(f"w2_landed{s}") for s in range(SLOTS)]
        hidden_ready, hidden_biased, gelu_ready = sem("hidden_ready"), sem("hidden_biased"), sem("gelu_ready")
        out_ready, out_copied, out_stored = sem("out_ready"), sem("out_copied"), sem("out_stored")

        with nc.Block() as block:
            @block.sync
            def _(sp):
                sp.sem_inc(out_ready, SLOTS)
                sp.sem_inc(out_copied, 2)
                with sp.Fori(0, EXPERTS // SLOTS, 1) as i:
                    for s in range(SLOTS):
                        sp.wait_ge(out_ready, i * SLOTS + s + 1)
                        sp.dma_start(w1[:, s], io["e_w1"][ds((i * SLOTS + s) * P, P), :]).then_inc(w1_landed[s], 16)
                        sp.dma_start(w2[:, s], io["e_w2"][ds((i * SLOTS + s) * P, P), :]).then_inc(w2_landed[s], 16)
                sp.wait_ge(out_copied, EXPERTS + 2)
                sp.dma_start(outE_dram, ob[:]).then_inc(out_stored, 16)
                sp.wait_ge(out_stored, 16)

            @block.tensor
            def _(pe):
                def first(i, s):
                    pe.wait_ge(w1_landed[s], 16 * i + 16)
                    for c in range(4):
                        mm = nc.tensor.matmul(ps1[s % 2][:, c, :], w1[:, s, c * P:(c + 1) * P],
                                              pooledT[:, :, ds(i * SLOTS + s, 1)].rearrange("p n e -> p (n e)"),
                                              start=True, stop=True)
                    mm.then_inc(hidden_ready, 1)

                def second(i, s):
                    pe.wait_ge(gelu_ready, i * SLOTS + s + 1)
                    pe.wait_ge(w2_landed[s], 16 * i + 16)
                    pe.wait_ge(out_copied, i * SLOTS + s + 1)
                    for c in range(4):
                        mm = nc.tensor.matmul(ps2[s % 2][:, 0:C], hT[:, s % 2, c, :], w2[:, s, c * C:(c + 1) * C],
                                              start=(c == 0), stop=(c == 3))
                    mm.then_inc(out_ready, 1)
                LAST = EXPERTS // SLOTS - 1
                first(0, 0)
                with pe.Fori(0, LAST, 1) as i:
                    for s in range(SLOTS):
                        first(i + (s + 1) // SLOTS, (s + 1) % SLOTS)
                        second(i, s)
                for s in range(SLOTS):
                    if s + 1 < SLOTS:
                        first(LAST, s + 1)
                    second(LAST, s)

            @block.vector
            def _(dve):
                def bias_hidden(i, s):
                    e = i * SLOTS + s
                    dve.wait_ge(hidden_ready, e + 1)
                    b = cst["e_b1"][:, ds(e * 4, 4)].unsqueeze(2).to_broadcast([P, 4, N])
                    nc.vector.tensor_tensor(h[:, s % 2], ps1[s % 2][:], b, ALU.add).then_inc(hidden_biased, 1)

                def bias_out(i, s):
                    e = i * SLOTS + s
                    dve.wait_ge(out_ready, e + SLOTS + 1)
                    nc.vector.tensor_tensor(ob[:, ds(e, 1), :].rearrange("p e c -> p (e c)"), ps2[s % 2][:, 0:C],
                                            cst["e_b2"][:, ds(e * C, C)], ALU.add).then_inc(out_copied, 1)
                LAST = EXPERTS // SLOTS - 1
                bias_hidden(0, 0)
                with dve.Fori(0, LAST, 1) as i:
                    for s in range(SLOTS):
                        bias_hidden(i + (s + 1) // SLOTS, (s + 1) % SLOTS)
                        bias_out(i, s)
                for s in range(SLOTS):
                    if s + 1 < SLOTS:
                        bias_hidden(LAST, s + 1)
                    bias_out(LAST, s)

            @block.scalar
            def _(act):
                with act.Fori(0, EXPERTS // SLOTS, 1) as i:
                    for s in range(SLOTS):
                        e = i * SLOTS + s
                        act.wait_ge(hidden_biased, e + 1)
                        nc.scalar.activation(hT[:, s % 2], h[:, s % 2], ACT.Gelu).then_inc(gelu_ready, 1)


def scatter_attention_route(nc, io, t1_dram, sel_dram, outE_dram, out_dram):
    with ExitStack() as ctx:
        def sb(name, shape, dt=F32):
            return ctx.enter_context(nc.sbuf_tensor(name, shape, dt))

        cst = load_constants(nc, ctx, io, ["router_w", "router_b", "iota8", "r_w", "r_b", "ident", "eps", "ones"], "p5")
        V1 = C + 1
        xin = sb("xin5", [TT, IT, C])
        xt = sb("xt5", [TT, IT, C])
        xprev = sb("xprev5", [TT, IT, C])
        sel = sb("sel5", [P, HW])
        oe = sb("oe5", [P, C])
        val = sb("val5", [TT, IT, V1])
        uT = sb("uT5", [P, CHUNKS * CT])
        sq = sb("sq5", [P, 2, CT])
        peak = sb("peak5", [P, CHUNKS * CT], BF16)
        minus1 = sb("minus1", [P, TT], BF16)
        uhi = sb("uhi5", [P, CHUNKS * CT], F16)
        ulo = sb("ulo5", [P, CHUNKS * CT], F16)
        E = sb("E5", [TT, 4, CT])
        st = sb("st5", [TT, IT, 6])
        mv = sb("mv5", [TT, IT, 2])
        rs = sb("rs5", [TT, IT])
        rden = sb("rden5", [TT, CH])
        lg = sb("lg5", [TT, IT, ROUTED])
        pr = sb("pr5", [TT, IT, ROUTED])
        red = sb("red5", [TT, IT])
        vals = sb("vals5", [TT, IT, 8])
        idx = sb("idx5", [TT, IT, 8], U32)
        idxf = sb("idxf5", [TT, IT, 8])
        share = sb("share5", [TT, IT, ROUTED])
        other = sb("other5", [TT, IT, ROUTED])
        prod = sb("prod5", [TT, 2, ROUTED, C])
        routed = sb("routed5", [TT, CH, C])
        shareT = sb("shareT5", [ROUTED, CHUNKS * CT])
        shareTc = sb("shareTc5", [P, CT])
        u4T = sb("u4T5", [P, CHUNKS * CT])
        u4Tc = sb("u4Tc5", [P, CT])
        bank = [ctx.enter_context(nc.psum_tensor(f"bank5_{k}", [P, 512], F32)) for k in range(8)]

        def sem(name, per=CHUNKS):
            return Turns(ctx.enter_context(nc.semaphore(name)), per)
        landed = sem("p5_landed", 48)
        stored = sem("p5_stored", 16)
        ones_set = sem("ones_set", 1)
        spread = sem("spread_ready5")
        added = sem("spread_added5")
        var_ready = sem("var5_ready", 2)
        std_ready = sem("std5_ready", 2)
        u_ready = sem("u5_ready")
        u_turned = sem("u5_turned")
        uT_ready = sem("uT5_ready")
        sq_ready = sem("sq_ready")
        uhi_ready = sem("uhi_ready")
        ulo_ready = sem("ulo_ready")
        norm_ready = sem("norm_ready")
        peak_ready = sem("peak_ready")
        score_ready = sem("score_ready", CHUNKS * IT)
        exp_ready = sem("exp5_ready", CHUNKS * IT)
        mix_step = sem("mix_step", CHUNKS * IT)
        mix_read = sem("mix_read")
        u4_ready = sem("u4_ready")
        u4_turned = sem("u4_turned")
        u4T_ready = sem("u4T_ready")
        route_ready = sem("route_ready", 1)
        lg_ready = sem("lg5_ready", 1)
        pr_ready = sem("pr5_ready", 1)
        share_ready = sem("share_ready", 1)
        share_turned = sem("share_turned")
        shareT_ready = sem("shareT_ready")
        chunk_placed = ctx.enter_context(nc.semaphore("chunk_placed"))
        bias_ready = ctx.enter_context(nc.semaphore("bias_ready"))
        bias_added = ctx.enter_context(nc.semaphore("bias_added"))
        expert_ready = ctx.enter_context(nc.semaphore("expert_ready"))
        expert_read = ctx.enter_context(nc.semaphore("expert_read"))
        mixed = ctx.enter_context(nc.semaphore("experts_mixed"))
        chunk_summed = ctx.enter_context(nc.semaphore("chunk_summed"))
        out_ready = ctx.enter_context(nc.semaphore("out5_ready"))
        xprev_ready = sem("xprev_ready", 1)
        chain = ctx.enter_context(nc.semaphore("dve5_step"))
        mix_chain = ctx.enter_context(nc.semaphore("mix_den_ready"))
        tick = ctx.enter_context(nc.semaphore("dve5_tick"))
        sp_tick = ctx.enter_context(nc.semaphore("sp5_tick"))
        pe_tick = ctx.enter_context(nc.semaphore("pe5_tick"))
        act_tick = ctx.enter_context(nc.semaphore("act5_tick"))

        with nc.Block() as block:
            @block.sync
            def _(sp):
                def load(n):
                    sp.dma_start(xin[:], image_view(t1_dram, n)).then_inc(landed.sem, 16)
                    sp.dma_start(sel[0:EXPERTS, :], sel_dram[ds(n * EXPERTS, EXPERTS), :]).then_inc(landed.sem, 16)
                    sp.dma_start(oe[0:EXPERTS, :], outE_dram[ds(n, 1)].rearrange("n e c -> (n e) c"))\
                        .then_inc(landed.sem, 16)

                def store(n):
                    sp.wait_ge(out_ready, n + 1)
                    sp.sem_inc(sp_tick, 1)
                    sp.dma_start(image_view(out_dram, n), xprev[:]).then_inc(stored.sem, 16)
                sp.wait_ge(ones_set.sem, 6)
                load(0)
                added.wait(sp, 0, CHUNKS)
                load(1)
                with sp.Fori(1, N - 1, 1) as n:
                    added.wait(sp, n, CHUNKS)
                    sp.sem_inc(sp_tick, 1)
                    load(n + 1)
                    store(n - 1)
                store(N - 2)
                store(N - 1)
                sp.wait_ge(stored.sem, 16 * N + 16)

            @block.gpsimd
            def _(pool):
                pool.sem_inc(stored.sem, 16)
                pool.memset(val[:, :, C:V1], 1.0).then_inc(ones_set.sem, 1)
                pool.memset(minus1[:], -1.0).then_inc(ones_set.sem, 1)
                pool.memset(sel[:], 0.0).then_inc(ones_set.sem, 1)
                pool.memset(oe[:], 0.0).then_inc(ones_set.sem, 1)
                pool.memset(shareTc[:], 0.0).then_inc(ones_set.sem, 1)
                pool.memset(peak[:], 0.0).then_inc(ones_set.sem, 1)

            @block.tensor
            def _(pe):
                pe.wait_ge(ones_set.sem, 6)
                def image(n, prev):
                    landed.wait(pe, n, 48)

                    def spread_out(j):
                        for a in range(CH):
                            t = j * CH + a
                            mm = nc.tensor.matmul(bank[j % 2][0:TT, a * C:(a + 1) * C], sel[:, t * TT:(t + 1) * TT],
                                                  oe[:], start=True, stop=True)
                        mm.then_inc(spread.sem, 1)

                    def norm_row(j):
                        sq_ready.wait(pe, n, j + 1)
                        nc.tensor.matmul(bank[4 + j % 2][0:1, 0:CT], cst["ones"][:, 0:1], sq[:, j % 2],
                                         start=True, stop=True).then_inc(norm_ready.sem, 1)
                    spread_out(0)
                    for j in range(CHUNKS):
                        if j + 1 < CHUNKS:
                            if j >= 1:
                                added.wait(pe, n, j)
                            spread_out(j + 1)
                    for j in range(CHUNKS):
                        u_ready.wait(pe, n, j + 1)
                        if j >= 2:
                            sq_ready.wait(pe, n, j - 1)
                        for a in range(CH):
                            tr = nc.tensor.transpose(bank[2 + j % 2][:, a * TT:(a + 1) * TT], val[:, j * CH + a, 0:C],
                                                     cst["ident"][0:TT, 0:TT])
                        tr.then_inc(u_turned.sem, 1)
                        norm_row(j)
                    peak_ready.wait(pe, n, CHUNKS)
                    ulo_ready.wait(pe, n, CHUNKS)
                    pe.sem_inc(pe_tick, 1)
                    with pe.Fori(0, CHUNKS, 1) as j:
                        base = (n * CHUNKS + j) * IT

                        def score(t, j=j):
                            for a, b in ((uhi, uhi), (uhi, ulo), (ulo, uhi)):
                                nc.tensor.matmul(bank[t % 4][0:TT, 0:CT], a[:, t * TT:(t + 1) * TT],
                                                 b[:, ds(j * CT, CT)], start=(a is b), stop=False)
                            nc.tensor.matmul(bank[t % 4][0:TT, 0:CT], minus1[:], peak[:, ds(j * CT, CT)],
                                             start=False, stop=True).then_inc(score_ready.sem, 1)
                        for t in range(3):
                            score(t)
                        for t in range(IT):
                            if t + 3 < IT:
                                score(t + 3)
                            pe.wait_ge(exp_ready.sem, base + t + 1)
                            if t == 0:
                                pe.wait_ge(mix_read.sem, n * CHUNKS + j + 1)
                            for a in range(CH):
                                mm = nc.tensor.matmul(bank[4 + a // 2][0:TT, (a % 2) * V1:(a % 2 + 1) * V1],
                                                      E[:, t % 4, a * TT:(a + 1) * TT], val[:, t, :],
                                                      start=(t == 0 and a % 2 == 0), stop=(t == IT - 1),
                                                      skip_group_check=True)
                            mm.then_inc(mix_step.sem, 1)
                            if prev and t == 3:
                                route_bias((n - 1) * CHUNKS + j)
                            if prev and t in (7, 12, 17, 22):
                                route((n - 1) * CHUNKS + j, (t - 7) // 5)
                    for j in range(CHUNKS):
                        u4_ready.wait(pe, n, j + 1)
                        if j >= 2:
                            u4T_ready.wait(pe, n, j - 1)
                        for a in range(CH):
                            tr = nc.tensor.transpose(bank[2 + j % 2][:, a * TT:(a + 1) * TT], val[:, j * CH + a, 0:C],
                                                     cst["ident"][0:TT, 0:TT])
                        tr.then_inc(u4_turned.sem, 1)
                    u4T_ready.wait(pe, n, CHUNKS)
                    for t in range(IT):
                        mm = nc.tensor.matmul(bank[1][0:TT, t * ROUTED:(t + 1) * ROUTED],
                                              u4T[:, t * TT:(t + 1) * TT], cst["router_w"][:], start=True, stop=True)
                    mm.then_inc(route_ready.sem, 1)

                    share_ready.wait(pe, n, 1)
                    for j in range(CHUNKS):
                        if j >= 2:
                            shareT_ready.wait(pe, n, j - 1)
                        for a in range(CH):
                            tr = nc.tensor.transpose(bank[2 + j % 2][0:ROUTED, a * TT:(a + 1) * TT],
                                                     share[:, j * CH + a, :], cst["ident"][0:TT, 0:TT])
                        tr.then_inc(share_turned.sem, 1)
                    shareT_ready.wait(pe, n, CHUNKS)
                    pe.sem_inc(pe_tick, 1)

                def route_bias(r):
                    pe.wait_ge(chunk_placed, 2 * r + 2)
                    pe.wait_ge(expert_read, CH * r + CH)
                    for a in range(CH):
                        mm = nc.tensor.matmul(bank[6][0:TT, a * C:(a + 1) * C], shareTc[:, a * TT:(a + 1) * TT],
                                              cst["r_b"][:], start=True, stop=True)
                    mm.then_inc(bias_ready, 1)

                def route(r, a):
                    if a == 0:
                        pe.wait_ge(bias_added, r + 1)
                    else:
                        pe.wait_ge(expert_read, CH * r + CH + a)
                    for k in range(2):
                        mm = nc.tensor.matmul(bank[6 + k][0:TT, 0:4 * C], u4Tc[:, a * TT:(a + 1) * TT],
                                              cst["r_w"][:, k * 4 * C:(k + 1) * 4 * C], start=True, stop=True)
                    mm.then_inc(expert_ready, 1)
                image(0, False)
                with pe.Fori(1, N, 1) as n:
                    image(n, True)
                with pe.Fori(0, CHUNKS, 1) as j:
                    route_bias((N - 1) * CHUNKS + j)
                    for a in range(CH):
                        route((N - 1) * CHUNKS + j, a)

            @block.scalar
            def _(act):
                S = nc.scalar
                def place(r, j):
                    act.wait_ge(expert_ready, CH * r + CH)
                    S.copy(u4Tc[:], u4T[:, ds(j * CT, CT)]).then_inc(chunk_placed, 1)
                    S.copy(shareTc[0:ROUTED, :], shareT[:, ds(j * CT, CT)]).then_inc(chunk_placed, 1)
                act.wait_ge(ones_set.sem, 6)

                def image(n, prev):
                    def root(k):
                        var_ready.wait(act, n, k)
                        S.activation(rs[:], mv[:, :, 1], ACT.Sqrt, bias=cst["eps"][0:TT, 0:1]).then_inc(std_ready.sem, 1)
                    root(1)
                    for j in range(CHUNKS):
                        u_turned.wait(act, n, j + 1)
                        S.copy(uT[:, j * CT:(j + 1) * CT], bank[2 + j % 2][:, 0:CT]).then_inc(uT_ready.sem, 1)
                        S.copy(uhi[:, j * CT:(j + 1) * CT], bank[2 + j % 2][:, 0:CT]).then_inc(uhi_ready.sem, 1)
                        S.activation(sq[:, j % 2], bank[2 + j % 2][:, 0:CT], ACT.Square).then_inc(sq_ready.sem, 1)
                        norm_ready.wait(act, n, j + 1)
                        S.copy(peak[0:1, j * CT:(j + 1) * CT], bank[4 + j % 2][0:1, 0:CT]).then_inc(peak_ready.sem, 1)
                    with act.Fori(0, CHUNKS, 1) as j:
                        base = (n * CHUNKS + j) * IT
                        if prev:
                            place((n - 1) * CHUNKS + j, j)
                        for t in range(IT):
                            act.wait_ge(score_ready.sem, base + t + 1)
                            act.wait_ge(mix_step.sem, base + t + 1)
                            S.activation(E[:, t % 4], bank[t % 4][0:TT, 0:CT], ACT.Exp)\
                                .then_inc(exp_ready.sem, 1)
                    root(2)
                    for j in range(CHUNKS):
                        u4_turned.wait(act, n, j + 1)
                        S.copy(u4T[:, j * CT:(j + 1) * CT], bank[2 + j % 2][:, 0:CT]).then_inc(u4T_ready.sem, 1)
                    lg_ready.wait(act, n, 1)
                    S.activation(pr[:], lg[:], ACT.Exp).then_inc(pr_ready.sem, 1)
                    for j in range(CHUNKS):
                        share_turned.wait(act, n, j + 1)
                        S.copy(shareT[:, j * CT:(j + 1) * CT], bank[2 + j % 2][0:ROUTED, 0:CT])\
                            .then_inc(shareT_ready.sem, 1)
                    shareT_ready.wait(act, n, CHUNKS)
                    act.sem_inc(act_tick, 1)
                image(0, False)
                with act.Fori(1, N, 1) as n:
                    image(n, True)
                with act.Fori(0, CHUNKS, 1) as j:
                    place((N - 1) * CHUNKS + j, j)

            @block.vector
            def _(dve):
                V = nc.vector
                dve.sem_inc(mix_read.sem, 1)
                dve.sem_inc(mix_step.sem, 4)
                cc = Chain(dve, chain, 0)
                dve.sem_inc(expert_ready, CH)
                dve.sem_inc(expert_read, CH)

                def route_bias(r, j):
                    dve.wait_ge(bias_ready, r + 1)
                    x = xprev[:, ds(j * CH, CH), :]
                    V.tensor_tensor(x, x, bank[6][0:TT, 0:CH * C].rearrange("p (a c) -> p a c", a=CH), ALU.add)\
                        .then_inc(bias_added, 1)

                def route(r, j):
                    for a in range(CH):
                        dve.wait_ge(expert_ready, CH * r + CH + a + 1)
                        if a >= 2:
                            dve.wait_ge(mixed, CH * r + a - 1)
                        for k in range(2):
                            w = share[:, ds(j * CH + a, 1), 4 * k:4 * k + 4].rearrange("p a e -> p (a e)")\
                                .unsqueeze(2).to_broadcast([TT, 4, C])
                            ins = V.tensor_tensor(prod[:, a % 2, 4 * k:4 * k + 4, :], bank[6 + k][0:TT, 0:4 * C]
                                                  .rearrange("p (e c) -> p e c", e=4), w, ALU.mult)
                        ins.then_inc(expert_read, 1)
                        dve.wait_ge(expert_read, CH * r + CH + a + 1)
                        V.tensor_reduce(routed[:, a, :], prod[:, a % 2].rearrange("p e c -> p c e"), AX.X, ALU.add)\
                            .then_inc(mixed, 1)
                    dve.wait_ge(mixed, CH * r + CH)
                    dve.wait_ge(bias_added, r + 1)
                    x = xprev[:, ds(j * CH, CH), :]
                    V.tensor_tensor(x, x, routed[:], ALU.add).then_inc(chunk_summed, 1)

                def image(n, prev):
                    cc.turn, cc.per, cc.k = n, P5_LINKS, 0

                    def norm(k, ready):
                        for t in range(IT):
                            ins = V.bn_stats(st[:, t], xt[:, t, :])
                        cc.link(ins)
                        dve.sem_inc(tick, 1)
                        for t in range(IT):
                            ins = V.bn_aggr(mv[:, t], st[:, t])
                        ins.then_inc(var_ready.sem, 1)
                        std_ready.wait(dve, n, k)
                        cc.link(V.reciprocal(rs[:], rs[:]))
                        for t in range(IT):
                            ins = V.tensor_scalar(val[:, t, 0:C], xt[:, t, :], mv[:, t, 0:1], rs[:, t:t + 1],
                                                  ALU.subtract, ALU.mult)
                            if t % CH == CH - 1:
                                ins.then_inc(ready.sem, 1)

                    for j in range(CHUNKS):
                        spread.wait(dve, n, j + 1)
                        V.tensor_tensor(xt[:, j * CH:(j + 1) * CH, :], xin[:, j * CH:(j + 1) * CH, :],
                                        bank[j % 2][0:TT, 0:CH * C].rearrange("p (a c) -> p a c", a=CH), ALU.add)\
                            .then_inc(added.sem, 1)
                    added.wait(dve, n, CHUNKS)
                    norm(1, u_ready)
                    for j in range(CHUNKS):
                        uhi_ready.wait(dve, n, j + 1)
                        uT_ready.wait(dve, n, j + 1)
                        cols = slice(j * CT, (j + 1) * CT)
                        V.tensor_tensor(ulo[:, cols], uT[:, cols], uhi[:, cols], ALU.subtract)\
                            .then_inc(ulo_ready.sem, 1)
                    with dve.Fori(0, CHUNKS, 1) as j:
                        if prev:
                            route_bias((n - 1) * CHUNKS + j, j)
                            route((n - 1) * CHUNKS + j, j)
                        dve.wait_ge(mix_step.sem, (n * CHUNKS + j + 1) * IT + 4)
                        q = n * CHUNKS + j
                        for k in range(2):
                            ins = V.reciprocal(rden[:, 2 * k:2 * k + 2], bank[4 + k][0:TT, 0:2 * V1]
                                               .rearrange("p (a c) -> p a c", a=2)[:, :, C])
                        ins.then_inc(mix_chain, 1)
                        dve.wait_ge(mix_chain, q + 1)
                        for a in range(CH):
                            x = xt[:, ds(j * CH + a, 1), :].rearrange("p a c -> p (a c)")
                            ins = V.scalar_tensor_tensor(x, bank[4 + a // 2][0:TT, (a % 2) * V1:(a % 2) * V1 + C],
                                                         rden[:, a:a + 1], x, ALU.mult, ALU.add)
                        ins.then_inc(mix_read.sem, 1)
                    dve.wait_ge(mix_read.sem, n * CHUNKS + CHUNKS + 1)
                    if prev:
                        dve.wait_ge(chunk_summed, n * CHUNKS)
                        dve.sem_inc(out_ready, 1)
                    norm(2, u4_ready)
                    rb = cst["router_b"][0:TT, :].unsqueeze(1).to_broadcast([TT, IT, ROUTED])

                    def wide(v):
                        return v.unsqueeze(2).to_broadcast([TT, IT, ROUTED])
                    route_ready.wait(dve, n, 1)
                    cc.link(V.tensor_tensor(lg[:], bank[1][0:TT, 0:IT * ROUTED].rearrange("p (a e) -> p a e", a=IT),
                                            rb, ALU.add))
                    cc.link(V.tensor_reduce(red[:], lg[:], AX.X, ALU.max))
                    V.tensor_tensor(lg[:], lg[:], wide(red[:]), ALU.subtract).then_inc(lg_ready.sem, 1)
                    pr_ready.wait(dve, n, 1)
                    cc.link(V.tensor_reduce(red[:], pr[:], AX.X, ALU.add))
                    cc.link(V.reciprocal(red[:], red[:]))
                    cc.link(V.tensor_tensor(pr[:], pr[:], wide(red[:]), ALU.mult))
                    dve.sem_inc(tick, 1)
                    for t in range(IT):
                        ins = V.max(vals[:, t], pr[:, t])
                    cc.link(ins)
                    dve.sem_inc(tick, 1)
                    for t in range(IT):
                        ins = V.max_index(idx[:, t], vals[:, t], pr[:, t])
                    cc.link(ins)
                    cc.link(V.tensor_copy(idxf[:], idx[:]))
                    cc.link(V.tensor_tensor(red[:], vals[:, :, 0], vals[:, :, 1], ALU.add))
                    cc.link(V.reciprocal(red[:], red[:]))
                    io8 = cst["iota8"][0:TT, :].unsqueeze(1).to_broadcast([TT, IT, ROUTED])
                    cc.link(V.tensor_tensor(share[:], io8, wide(idxf[:, :, 0]), ALU.is_equal))
                    cc.link(V.tensor_tensor(share[:], share[:], wide(vals[:, :, 0]), ALU.mult))
                    cc.link(V.tensor_tensor(other[:], io8, wide(idxf[:, :, 1]), ALU.is_equal))
                    cc.link(V.tensor_tensor(other[:], other[:], wide(vals[:, :, 1]), ALU.mult))
                    cc.link(V.tensor_tensor(share[:], share[:], other[:], ALU.add))
                    V.tensor_tensor(share[:], share[:], wide(red[:]), ALU.mult).then_inc(share_ready.sem, 1)
                    share_ready.wait(dve, n, 1)
                    stored.wait(dve, n, 16)
                    V.tensor_copy(xprev[:], xt[:]).then_inc(xprev_ready.sem, 1)
                    xprev_ready.wait(dve, n, 1)
                    dve.sem_inc(tick, 1)
                    assert cc.k == P5_LINKS, cc.k
                image(0, False)
                with dve.Fori(1, N, 1) as n:
                    image(n, True)
                with dve.Fori(0, CHUNKS, 1) as j:
                    route_bias((N - 1) * CHUNKS + j, j)
                    route((N - 1) * CHUNKS + j, j)
                dve.wait_ge(chunk_summed, N * CHUNKS)
                dve.sem_inc(out_ready, 1)



def build(nc, io, out):
    def dram(name, shape):
        return nc.dram_tensor(name, shape, F32, kind="Internal").ap()
    flat_out = out.rearrange("a b c d -> (a b c) d")
    patch_table = dram("patch_table", [N * POS, GROUPS * 4 * CG])
    feat_dram = dram("features", [C, T])
    x2_dram, t1_dram = dram("x2_dram", [T, C]), dram("t1_dram", [T, C])
    sel_dram, outE_dram = dram("sel_dram", [N * EXPERTS, HW]), dram("outE_dram", [N, EXPERTS, C])
    patches_and_features(nc, io, patch_table, feat_dram)
    deformable_and_mlp(nc, io, patch_table, feat_dram, x2_dram)
    with nc.sbuf_tensor("pooledT", [P, N, EXPERTS], F32) as pooledT:
        norm_conv_attention_gate(nc, io, pooledT, x2_dram, t1_dram, sel_dram)
        pooled_experts(nc, io, pooledT, outE_dram)
    scatter_attention_route(nc, io, t1_dram, sel_dram, outE_dram, flat_out)


def lay_out(np, a):
    f = np.float32
    x = a["x"]

    def rows(v, k=P):
        return np.broadcast_to(v.reshape(1, -1), (k, v.size))

    def cols(v):
        return v.reshape(-1, P).T
    io = {}
    xT = np.zeros((N, C, XPAD), f)
    xT[:, :, :WP * WP] = np.pad(x, ((0, 0), (1, 1), (1, 1), (0, 0))).transpose(0, 3, 1, 2).reshape(N, C, WP * WP)
    io["xT"] = xT
    io["x"] = x.reshape(T, C)
    io["ident"] = np.eye(P, dtype=f)
    io["eps"] = np.full((P, 1), 1e-5, f)
    L = {k[8:]: v for k, v in a.items() if k.startswith("L0_conv_")}
    io["w_in"] = L["w_in"]
    bias4 = np.zeros((4, 4 * C), f)
    for k in range(4):
        bias4[k, k * C:(k + 1) * C] = L["b_in"]
    io["bias_in12"] = np.tile(bias4, (3, 1))
    io["part12"] = np.repeat(np.eye(3, dtype=f), 4, axis=0)
    inside = np.zeros(XPAD, f)
    inside[:WP * WP] = np.pad(np.ones((H, W), f), 1).reshape(-1)
    io["interior12"] = np.tile(np.stack([inside[c:c + POS] for c in CORNER]), (3, 1))
    io["dw_w"] = L["dw_w"].reshape(C, 9)
    for k in ("dw_b", "bn_g", "bn_b", "bn_m", "bn_v"):
        io[k] = L[k].reshape(C, 1)
    io["w_om"] = np.concatenate([L["w_off"], L["w_msk"]], 1)
    io["b_om"] = rows(np.concatenate([L["b_off"], L["b_msk"]]))
    grid = np.zeros((GROUPS, POINTS, 2), f)
    grid[:, :, 0] = np.arange(POINTS) // 3 - 1
    grid[:, :, 1] = np.arange(POINTS) % 3 - 1
    io["grid"] = rows(np.concatenate([grid.reshape(-1), np.zeros(GP, f)]))
    tok = np.arange(T).reshape(TILES, P).T
    io["tok_base"] = (np.stack([tok % W, tok // W % H], -1) + 0.5).astype(f).reshape(P, TILES * 2)
    io["row_base"] = (tok // HW * (POS * GROUPS)).astype(f)
    io["group_col"] = rows(np.repeat(np.arange(GROUPS), POINTS).astype(f))
    io["w_out"] = L["w_out"]
    for k in ("b_out", "ln1_g", "ln1_b", "gamma1", "b_fc2", "ln2_g", "ln2_b", "gamma2"):
        io[k] = rows(L[k])
    io["w_fc1"] = L["w_fc1"]
    io["b_fc1"] = cols(L["b_fc1"])
    io["w_fc2"] = L["w_fc2"].reshape(4, P, C).transpose(1, 0, 2).reshape(P, 4 * C)
    io["kernelT"] = a["L1_conv_kernel"].reshape(9, C, C).transpose(2, 0, 1).reshape(C, 9 * C)
    io["conv_bias"] = a["L1_conv_bias"].reshape(C, 1)
    io["W"] = a["L1_conv_W"]
    io["group_avg"] = np.kron(np.eye(32), np.full((4, 4), 0.25)).astype(f)
    for k in "qkv":
        io["W" + k] = a["L2_attn_W" + k]
        io["b" + k] = a["L2_attn_b" + k].reshape(C, 1)
    io["gate_wT"] = a["L2_ffn_gate_w"].T
    io["gate_b"] = a["L2_ffn_gate_b"].reshape(EXPERTS, 1)
    w1, w2 = a["L2_ffn_weight1"], a["L2_ffn_weight2"]
    io["e_w1"] = w1[:, :C].reshape(EXPERTS * C, HID)
    io["e_b1"] = w1[:, C].reshape(EXPERTS, 4, P).transpose(2, 0, 1).reshape(P, EXPERTS * 4)
    io["e_w2"] = w2[:, :HID].reshape(EXPERTS, 4, P, C).transpose(0, 2, 1, 3).reshape(EXPERTS * P, 4 * C)
    io["e_b2"] = rows(w2[:, HID], N)
    io["router_w"] = a["L3_ffn_router_w"]
    io["router_b"] = rows(a["L3_ffn_router_b"])
    io["iota8"] = rows(np.arange(ROUTED, dtype=f))
    io["r_w"] = a["L3_ffn_expert_w"].transpose(1, 0, 2).reshape(C, ROUTED * C)
    io["r_b"] = np.concatenate([a["L3_ffn_expert_b"], np.zeros((P - ROUTED, C), f)])
    io["ones"] = np.ones((P, 1), f)
    return {k: np.ascontiguousarray(v) for k, v in io.items()}


def kernel(**inputs):
    import numpy as _np
    import concourse.bacc as _bacc
    from concourse import mybir as _mybir
    from concourse.bass_utils import run_bass_kernel_spmd as _run

    nc = _bacc.Bacc("TRN2", target_bir_lowering=False, num_devices=1)
    laid = lay_out(_np, {k: _np.asarray(v) for k, v in inputs.items()})
    arrays, io = {}, {}
    for name, a in laid.items():
        arrays[f"in_{name}"] = a
        io[name] = nc.dram_tensor(f"in_{name}", a.shape, _mybir.dt.from_np(a.dtype), kind="ExternalInput").ap()
    out = nc.dram_tensor("out_0_dram", (N, H, W, C), _mybir.dt.float32, kind="ExternalOutput").ap()
    build(nc, io, out)
    r = _run(nc, [arrays], core_ids=[0])
    return r.results[0]["out_0_dram"]
```
